# Optimizing a Trainium2 kernel written in Bass

```python
import numpy as np
import jax
import jax.numpy as jnp

def _softmax(x, axis=-1):
    return jax.nn.softmax(x, axis=axis)
def _gelu(x):
    return jax.nn.gelu(x, approximate=True)
def _silu(x):
    return jax.nn.silu(x)
def _sigmoid(x):
    return jax.nn.sigmoid(x)
def _layernorm(x, axis=-1, eps=1e-5):
    m = jnp.mean(x, axis=axis, keepdims=True)
    v = jnp.var(x, axis=axis, keepdims=True)
    return (x - m) / jnp.sqrt(v + eps)
def _scatter_add(tgt, idx, src, axis=0):
    return tgt.at[idx].add(src)
def _segment_sum(src, seg, n):
    return jax.ops.segment_sum(src, seg, n)

kernel_name = 'mk_conv_preact_d2_conv_nhwc96_ab3936'

def setup_inputs(seed: int = 0):
    np.random.seed(seed)
    _w = jnp.asarray
    def _rec_inputs():
        import jax
        import jax.numpy as jnp
        _gk = jax.random.key(seed)
        x = -0.0001538 + 1 * jax.random.normal(jax.random.fold_in(_gk, 1), (16, 64, 64, 96), jnp.float32)
        return x
    x = _rec_inputs()
    def _L0_conv_setup():
        import jax, jax.numpy as jnp
        import numpy as np
        UP = 2

        def _rect_1d(N, cutoff, edge_val):
            lo = int(N * cutoff // 2)
            hi = int(N - lo)
            r = np.ones(N, dtype=np.float32)
            r[lo + 1:hi] = 0.0
            if cutoff * N % 2 == 0:
                r[lo] = edge_val
                r[hi] = edge_val
            return r

        def _rect_mask_rfft(N, cutoff, edge_val):
            r = _rect_1d(N, cutoff, edge_val)
            m = r[:, None] * r[None, :]
            return jnp.asarray(m[:, :N // 2 + 1])

        def _upsample_rfft(x):
            B, C, H, W = x.shape
            z = jnp.zeros((B, C, H, UP, W, UP), x.dtype)
            z = z.at[:, :, :, 0, :, 0].set(x)
            xu = z.reshape(B, C, H * UP, W * UP)
            mask = _rect_mask_rfft(W * UP, 1.0 / UP, 1.0)
            xf = jnp.fft.rfft2(xu) * (UP * UP) * mask
            return jnp.fft.irfft2(xf, s=(H * UP, W * UP)).astype(x.dtype)

        def _lpf_rfft(x, cutoff=0.5):
            H, W = (x.shape[-2], x.shape[-1])
            mask = _rect_mask_rfft(W, cutoff, 0.5)
            xf = jnp.fft.rfft2(x) * mask
            return jnp.fft.irfft2(xf, s=(H, W)).astype(x.dtype)
        key = jax.random.key(seed)
        ks = jax.random.split(key, 6)
        B, H, W, dim = (16, 64, 64, 96)
        hidden = 4 * dim
        x = jax.random.normal(ks[0], (B, H, W, dim), jnp.float32)
        W1 = jax.random.normal(ks[1], (hidden, dim), jnp.float32) * 0.02
        b1 = jnp.zeros((hidden,), jnp.float32)
        W2 = jax.random.normal(ks[2], (dim, hidden), jnp.float32) * 0.02
        b2 = jnp.zeros((dim,), jnp.float32)
        init_coef = jnp.asarray([0.0169394634313126, 0.5, 0.3078363963999393], jnp.float32)
        coef = jnp.tile(init_coef[None, :], (hidden, 1))
        return {'x': x, 'W1': W1, 'b1': b1, 'W2': W2, 'b2': b2, 'coef': coef}
    _L0_conv_all = _L0_conv_setup()
    _L0_conv_in = {k: v for k, v in _L0_conv_all.items() if k in ('W1', 'b1', 'W2', 'b2', 'coef', )}
    del _L0_conv_all

    def _L1_conv_setup():
        import jax, jax.numpy as jnp
        import numpy as np

        def _mamba(u, W_in, conv_w, conv_b, W_x, W_dt, b_dt, A_log, D, W_out):
            Bsz, L, _ = u.shape
            d_inner, d_conv = conv_w.shape
            dt_rank = W_dt.shape[1]
            d_state = A_log.shape[1]
            xz = jnp.einsum('blc,ec->ble', u, W_in)
            xs, z = jnp.split(xz, 2, axis=-1)
            xp = jnp.pad(xs, ((0, 0), (d_conv - 1, 0), (0, 0)))
            xc = sum((xp[:, k:k + L, :] * conv_w[:, k] for k in range(d_conv))) + conv_b
            xc = jax.nn.silu(xc)
            dbc = jnp.einsum('bld,ed->ble', xc, W_x)
            dt = dbc[..., :dt_rank]
            Bm = dbc[..., dt_rank:dt_rank + d_state]
            Cm = dbc[..., dt_rank + d_state:]
            delta = jax.nn.softplus(jnp.einsum('blr,dr->bld', dt, W_dt) + b_dt)
            A = -jnp.exp(A_log)
            dA = jnp.exp(delta[..., None] * A)
            dBu = delta[..., None] * Bm[:, :, None, :] * xc[..., None]

            def step(h, inp):
                dA_t, dBu_t, C_t = inp
                h = dA_t * h + dBu_t
                y = jnp.einsum('bdn,bn->bd', h, C_t)
                return (h, y)
            h0 = jnp.zeros((Bsz, d_inner, d_state), u.dtype)
            _, ys = jax.lax.scan(step, h0, (jnp.swapaxes(dA, 0, 1), jnp.swapaxes(dBu, 0, 1), jnp.swapaxes(Cm, 0, 1)))
            y = jnp.swapaxes(ys, 0, 1) + xc * D
            y = y * jax.nn.silu(z)
            return jnp.einsum('bld,cd->blc', y, W_out)
        key = jax.random.key(seed)
        ks = jax.random.split(key, 8)
        B, H, W, d_model = (2, 96, 96, 96)
        d_state, d_conv, expand = (16, 3, 2)
        d_inner = expand * d_model
        dt_rank = -(-d_model // 16)
        x = jax.random.normal(ks[0], (B, H, W, d_model), jnp.float32)
        W_in = jax.random.normal(ks[1], (2 * d_inner, d_model), jnp.float32) * d_model ** (-0.5)
        conv_w = jax.random.normal(ks[2], (d_inner, d_conv), jnp.float32) * d_conv ** (-0.5)
        conv_b = jnp.zeros((d_inner,), jnp.float32)
        W_x = jax.random.normal(ks[3], (dt_rank + 2 * d_state, d_inner), jnp.float32) * d_inner ** (-0.5)
        W_dt = jax.random.normal(ks[4], (d_inner, dt_rank), jnp.float32) * dt_rank ** (-0.5)
        b_dt = jnp.log(jnp.expm1(jnp.full((d_inner,), 0.01, jnp.float32)))
        A_log = jnp.log(jnp.broadcast_to(jnp.arange(1, d_state + 1, dtype=jnp.float32), (d_inner, d_state)))
        D = jnp.ones((d_inner,), jnp.float32)
        W_out = jax.random.normal(ks[5], (d_model, d_inner), jnp.float32) * d_inner ** (-0.5)
        return {'x': x, 'W_in': W_in, 'conv_w': conv_w, 'conv_b': conv_b, 'W_x': W_x, 'W_dt': W_dt, 'b_dt': b_dt, 'A_log': A_log, 'D': D, 'W_out': W_out}
    _L1_conv_all = _L1_conv_setup()
    _L1_conv_in = {k: v for k, v in _L1_conv_all.items() if k in ('W_in', 'conv_w', 'conv_b', 'W_x', 'W_dt', 'b_dt', 'A_log', 'D', 'W_out', )}
    del _L1_conv_all

    return {
        "x": x,
        "L0_conv_W1": _L0_conv_in["W1"],
        "L0_conv_b1": _L0_conv_in["b1"],
        "L0_conv_W2": _L0_conv_in["W2"],
        "L0_conv_b2": _L0_conv_in["b2"],
        "L0_conv_coef": _L0_conv_in["coef"],
        "L1_conv_W_in": _L1_conv_in["W_in"],
        "L1_conv_conv_w": _L1_conv_in["conv_w"],
        "L1_conv_conv_b": _L1_conv_in["conv_b"],
        "L1_conv_W_x": _L1_conv_in["W_x"],
        "L1_conv_W_dt": _L1_conv_in["W_dt"],
        "L1_conv_b_dt": _L1_conv_in["b_dt"],
        "L1_conv_A_log": _L1_conv_in["A_log"],
        "L1_conv_D": _L1_conv_in["D"],
        "L1_conv_W_out": _L1_conv_in["W_out"],
    }

def reference(x, L0_conv_W1, L0_conv_b1, L0_conv_W2, L0_conv_b2, L0_conv_coef, L1_conv_W_in, L1_conv_conv_w, L1_conv_conv_b, L1_conv_W_x, L1_conv_W_dt, L1_conv_b_dt, L1_conv_A_log, L1_conv_D, L1_conv_W_out):
    import jax
    import jax.numpy as jnp
    def _L0_conv_ref(x, W1, b1, W2, b2, coef):
        import jax, jax.numpy as jnp
        import numpy as np
        UP = 2

        def _rect_1d(N, cutoff, edge_val):
            lo = int(N * cutoff // 2)
            hi = int(N - lo)
            r = np.ones(N, dtype=np.float32)
            r[lo + 1:hi] = 0.0
            if cutoff * N % 2 == 0:
                r[lo] = edge_val
                r[hi] = edge_val
            return r

        def _rect_mask_rfft(N, cutoff, edge_val):
            r = _rect_1d(N, cutoff, edge_val)
            m = r[:, None] * r[None, :]
            return jnp.asarray(m[:, :N // 2 + 1])

        def _upsample_rfft(x):
            B, C, H, W = x.shape
            z = jnp.zeros((B, C, H, UP, W, UP), x.dtype)
            z = z.at[:, :, :, 0, :, 0].set(x)
            xu = z.reshape(B, C, H * UP, W * UP)
            mask = _rect_mask_rfft(W * UP, 1.0 / UP, 1.0)
            xf = jnp.fft.rfft2(xu) * (UP * UP) * mask
            return jnp.fft.irfft2(xf, s=(H * UP, W * UP)).astype(x.dtype)

        def _lpf_rfft(x, cutoff=0.5):
            H, W = (x.shape[-2], x.shape[-1])
            mask = _rect_mask_rfft(W, cutoff, 0.5)
            xf = jnp.fft.rfft2(x) * mask
            return jnp.fft.irfft2(xf, s=(H, W)).astype(x.dtype)
        xc = jnp.transpose(x, (0, 3, 1, 2))
        xu = _upsample_rfft(xc)
        h = jnp.transpose(xu, (0, 2, 3, 1))
        h = h @ W1.T + b1
        h = coef[:, 0] + coef[:, 1] * h + coef[:, 2] * (h * h)
        h = h @ W2.T + b2
        hc = jnp.transpose(h, (0, 3, 1, 2))
        hl = _lpf_rfft(hc, cutoff=0.5)
        out = hl[:, :, ::2, ::2]
        return jnp.transpose(out, (0, 2, 3, 1))

    def _L1_conv_ref(x, W_in, conv_w, conv_b, W_x, W_dt, b_dt, A_log, D, W_out):
        import jax, jax.numpy as jnp
        import numpy as np

        def _mamba(u, W_in, conv_w, conv_b, W_x, W_dt, b_dt, A_log, D, W_out):
            Bsz, L, _ = u.shape
            d_inner, d_conv = conv_w.shape
            dt_rank = W_dt.shape[1]
            d_state = A_log.shape[1]
            xz = jnp.einsum('blc,ec->ble', u, W_in)
            xs, z = jnp.split(xz, 2, axis=-1)
            xp = jnp.pad(xs, ((0, 0), (d_conv - 1, 0), (0, 0)))
            xc = sum((xp[:, k:k + L, :] * conv_w[:, k] for k in range(d_conv))) + conv_b
            xc = jax.nn.silu(xc)
            dbc = jnp.einsum('bld,ed->ble', xc, W_x)
            dt = dbc[..., :dt_rank]
            Bm = dbc[..., dt_rank:dt_rank + d_state]
            Cm = dbc[..., dt_rank + d_state:]
            delta = jax.nn.softplus(jnp.einsum('blr,dr->bld', dt, W_dt) + b_dt)
            A = -jnp.exp(A_log)
            dA = jnp.exp(delta[..., None] * A)
            dBu = delta[..., None] * Bm[:, :, None, :] * xc[..., None]

            def step(h, inp):
                dA_t, dBu_t, C_t = inp
                h = dA_t * h + dBu_t
                y = jnp.einsum('bdn,bn->bd', h, C_t)
                return (h, y)
            h0 = jnp.zeros((Bsz, d_inner, d_state), u.dtype)
            _, ys = jax.lax.scan(step, h0, (jnp.swapaxes(dA, 0, 1), jnp.swapaxes(dBu, 0, 1), jnp.swapaxes(Cm, 0, 1)))
            y = jnp.swapaxes(ys, 0, 1) + xc * D
            y = y * jax.nn.silu(z)
            return jnp.einsum('bld,cd->blc', y, W_out)
        B, H, W, C = x.shape
        y = _mamba(x.reshape(B, H * W, C), W_in, conv_w, conv_b, W_x, W_dt, b_dt, A_log, D, W_out)
        return y.reshape(B, H, W, C)

    def _gn(v, G=32, eps=1e-5):
        B_, H_, W_, C_ = v.shape
        g = v.reshape(B_, H_, W_, G, C_ // G)
        m = jnp.mean(g, axis=(1, 2, 4), keepdims=True)
        s = jnp.var(g, axis=(1, 2, 4), keepdims=True)
        return ((g - m) / jnp.sqrt(s + eps)).reshape(v.shape)

    def _ln_c(v, eps=1e-6):
        m = jnp.mean(v, axis=-1, keepdims=True)
        s = jnp.var(v, axis=-1, keepdims=True)
        return (v - m) / jnp.sqrt(s + eps)

    def _ln_t(v, eps=1e-5):
        m = jnp.mean(v, axis=-1, keepdims=True)
        s = jnp.var(v, axis=-1, keepdims=True)
        return (v - m) / jnp.sqrt(s + eps)

    def _to_tokens(v):
        B_, H_, W_, C_ = v.shape
        return v.reshape(B_, H_ * W_, C_)
    def _from_tokens(t, like):
        return t.reshape(like.shape)

    x = x + _L0_conv_ref(_gn(x), L0_conv_W1, L0_conv_b1, L0_conv_W2, L0_conv_b2, L0_conv_coef)
    x = x + _L1_conv_ref(_gn(x), L1_conv_W_in, L1_conv_conv_w, L1_conv_conv_b, L1_conv_W_x, L1_conv_W_dt, L1_conv_b_dt, L1_conv_A_log, L1_conv_D, L1_conv_W_out)
    return x


_drawn_inputs = setup_inputs


def setup_inputs(seed=0):
    import zlib

    import numpy as np

    out = dict(_drawn_inputs(seed))
    spreads = {'L0_conv_b1': (0.0, 0.342),
     'L0_conv_b2': (0.0, 0.1),
     'L1_conv_conv_b': (0.0, 0.1),
     'L1_conv_b_dt': (-4.600166320800781, 0.6),
     'L1_conv_D': (1.0, 0.2)}
    factors = {}
    for name, (base, spread) in spreads.items():
        noise = np.random.default_rng([zlib.crc32(name.encode()), seed]).standard_normal(out[name].shape)
        drawn = base * np.exp(spread * noise) if base else spread * noise
        out[name] = jnp.asarray(drawn.astype(out[name].dtype))
    for name, factor in factors.items():
        out[name] = (out[name] * factor).astype(out[name].dtype)
    return out
```

```python
from contextlib import ExitStack

import numpy as np

import concourse.bass as bass
from concourse import mybir

F32 = mybir.dt.float32
BF16 = mybir.dt.bfloat16
ALU = mybir.AluOpType
ACT = mybir.ActivationFunctionType

NS, HH, WW, C = 16, 64, 64, 96
L = HH * WW
GROUP = 3
HID = 384
NF = HID // 128
GW, GH = 100, 98
NB = GW // 4
BC = 4 * GH
DI, DSTATE, RANK = 192, 16, 6
T = 512
NC8 = L // T
NJ, NQ = DI // 32, DSTATE // 4
NU = NJ * NQ
XB_H = 8
LEAD = 2


def s_steps():
    out = []
    for b in range(HH // XB_H):
        out += [("ST", b), ("SA", b), ("SB", b)]
    return out + [("SG1", 0), ("SG2", 0)]


def w_steps():
    out = [("WG", 0)]
    for b in range(NB + 3):
        if b < NB:
            out.append(("W_up", b))
        if 1 <= b <= NB:
            out += [("W_f", b - 1, f) for f in range(NF)]
        if 2 <= b <= NB + 1:
            out.append(("W_2", b - 2))
        if b >= 3:
            out.append(("W_dn", b - 3))
    return out + [("WPAD", 0)]


def d_steps():
    out = [("DG", 0), ("D_xt", 0)]
    for k in range(NC8):
        if k + 1 < NC8:
            out.append(("D_xt", k + 1))
        out += [("D_lo", k), ("D_hi", k)]
    return out + [("DG1", 0), ("DG2", 0), ("DPAD", 0)]


def merged(d, w, s):
    rows = []
    for use, steps, end in ((d, d_steps(), 0.62), (w, w_steps(), 1.0), (s, s_steps(), 1.0)):
        if use:
            n = len(steps)
            rows += [((i / n) * end, st) for i, st in enumerate(steps)]
    rows.sort(key=lambda r: r[0])
    return [(int(p * NC8 * NU), st) for p, st in rows]


def build(nc, A):
    ctx = ExitStack()
    with ctx:
        def sb(name, shape, dt=F32):
            return ctx.enter_context(nc.sbuf_tensor(name, shape, dt))

        def ps(name, shape):
            return ctx.enter_context(nc.psum_tensor(name, shape, F32))

        def sem(name):
            return ctx.enter_context(nc.semaphore(name))

        t1_d = nc.dram_tensor("t1_scratch", [NS, GW, HH * C], F32, kind="Internal").ap()
        v2_d = nc.dram_tensor("v2_scratch", [NS, HH, GW, C], F32, kind="Internal").ap()
        x1_d = nc.dram_tensor("x1_scratch", [NS, C, L], F32, kind="Internal").ap()
        dl_d = nc.dram_tensor("delta_scratch", [2, DI, T], F32, kind="Internal").ap()
        du_d = nc.dram_tensor("deltax_scratch", [2, DI, T], F32, kind="Internal").ap()

        up_w = sb("up_w", [128, 2, GW])
        up_h = sb("up_h", [128, 2 * GH])
        dn_h = sb("dn_h", [GH, HH])
        dn_w = sb("dn_w", [GW, 96])
        ident = sb("ident", [128, 128])
        gavg = sb("gavg", [C, C])
        w1t = sb("w1t", [C, HID])
        w1a = sb("w1a", [C, HID])
        w2c = sb("w2c", [128, NF, C])
        b1t = sb("b1t", [128, NF])
        coef = sb("coef", [128, NF, 3])
        fcst = sb("fcst", [128, NF])
        b2t = sb("b2t", [C, 1])
        wlin = sb("wlin", [C, C])
        wtot = sb("wtot", [C, C])
        cbase = sb("cbase", [C, 1])
        win = sb("win", [C, 2 * DI])
        tapw = sb("tapw", [C + 1, 3, DI])
        wx = sb("wx", [C, 2, C])
        wdt = sb("wdt", [C + 1, DI])
        wo = sb("wo", [C, 2, C])
        nega = sb("nega", [128, NQ, NJ])
        dhalf = sb("dhalf", [C, 2])
        selb = sb("selb", [C, 2 * NQ, 128], BF16)
        rsel = sb("rsel", [128, 32])

        xb = sb("xb", [128, 2, 4, C])
        t1s = sb("t1s", [GW, 2, XB_H, C])
        t1r = sb("t1r", [128, 2, 5, C])
        xu = sb("xu", [C, 2, BC])
        g2 = sb("g2", [128, 2, NF, BC])
        vr = sb("vr", [GH, 2, 4 * C])
        v2s = sb("v2s", [HH, 2, 4 * C])
        rr = sb("rr", [GW, 2, 4, C])
        xp = sb("xp", [128, 2, 4, C])
        xt = sb("xt", [C, 2, T])
        x1s = sb("x1s", [C, 2, T])
        bst = sb("bst", [C, 2, 8, 6])
        mv = sb("mv", [C, 2, 2])
        mg = sb("mg", [C, 2])
        dm = sb("dm", [C, 2])
        vv = sb("vv", [C, 2])
        ve = sb("ve", [C, 2])
        mhalf = sb("mhalf", [C, 1])
        zero2 = sb("zero2", [C, 2])
        gnx = sb("gnx", [C, 2])
        gnd = sb("gnd", [C, 2])
        gn1 = sb("gn1", [C, 2])
        gna = sb("gna", [C, 2])
        b1a = sb("b1a", [128, NF])
        cst = sb("cst", [C, 1])

        x1c = sb("x1c", [C, 4, T])
        xn = sb("xn", [C + 1, 4, T + 2])
        xcs = sb("xcs", [C, 4, 2, T])
        zs = sb("zs", [C, 2, T])
        t0 = sb("t0", [C, 2, T])
        t1 = sb("t1", [C, 2, T])
        t2 = sb("t2", [C, 2, T])
        dbc = sb("dbc", [C + 1, T])
        bc3 = sb("bc3", [C, 4, T], BF16)
        rep_d = sb("rep_d", [128, 2, NJ, T])
        rep_u = sb("rep_u", [128, 2, NJ, T])
        cs = sb("cs", [128, 2, T])
        av = sb("av", [128, 4, T])
        bu = sb("bu", [128, 4, 2, T])
        hc = sb("hc", [128, 4, T])
        w2t = hc[:, 0, 0:NF * C].rearrange("p (f c) -> p f c", f=NF)
        state = sb("state", [128, NQ, NJ])
        yy = sb("yy", [C, 2, T])
        os_ = sb("os_", [128, 2, 4, C])

        cb = ps("cb", [128, 2, 512])
        px = ps("px", [128, 2, 512])
        pb = ps("pb", [128, 512])
        pm = ps("pm", [128, 512])
        py = ps("py", [128, 2, 512])

        ld_w = sem("ld_w")
        sp_passed = sem("sp_passed")
        zset = sem("zset")
        setup_v = sem("setup_v")
        setup_a = sem("setup_a")
        pe_conv = sem("pe_conv")
        cb_free = [sem("cb_free0"), sem("cb_free1")]
        xb_ld = [sem("xb_ld0"), sem("xb_ld1")]
        t1_st = [sem("t1_st0"), sem("t1_st1")]
        t1_ld = [sem("t1_ld0"), sem("t1_ld1")]
        v2_st = [sem("v2_st0"), sem("v2_st1")]
        rr_ld = [sem("rr_ld0"), sem("rr_ld1")]
        xp_ld = [sem("xp_ld0"), sem("xp_ld1")]
        x1_st = [sem("x1_st0"), sem("x1_st1")]
        dve_s = sem("dve_s")
        dve_w = sem("dve_w")
        dve_d = sem("dve_d")
        x1_bn = sem("x1_bn")
        pool_s = sem("pool_s")
        pool_d = sem("pool_d")
        act_gn = sem("act_gn")
        x1c_ld = [sem(f"x1c_ld{i}") for i in range(4)]
        act_halo = sem("act_halo")
        act_xn = sem("act_xn")
        pe_x = sem("pe_x")
        act_tx = sem("act_tx")
        dve_xcs = sem("dve_xcs")
        pe_z = sem("pe_z")
        act_tz = sem("act_tz")
        dve_zs = sem("dve_zs")
        pe_dbc = sem("pe_dbc")
        act_dbc = sem("act_dbc")
        dve_bc = sem("dve_bc")
        pe_dt = sem("pe_dt")
        act_sp = sem("act_sp")
        dve_sp = sem("dve_sp")
        pool_sp = sem("pool_sp")
        dl_st = sem("dl_st")
        du_st = sem("du_st")
        rd_ld = [sem("rd_ld0"), sem("rd_ld1")]
        ru_ld = [sem("ru_ld0"), sem("ru_ld1")]
        pe_b = sem("pe_b")
        pe_c = sem("pe_c")
        act_c = sem("act_c")
        act_a = sem("act_a")
        dve_bu = sem("dve_bu")
        dve_h = sem("dve_h")
        dve_stt = sem("dve_stt")
        pool_hc = sem("pool_hc")
        pe_red = sem("pe_red")
        dve_y = sem("dve_y")
        pe_out = sem("pe_out")
        act_out = sem("act_out")
        out_st = [sem("out_st0"), sem("out_st1")]

        xtok = A["x"].rearrange("s h w c -> s (h w) c")
        otok = A["out"].rearrange("s h w c -> s (h w) c")

        def tok(ap, s, t0_, n):
            v = ap[bass.ds(val(s), 1), t0_:t0_ + n, :].rearrange("o t c -> (o t) c")
            return v.rearrange("(i p) c -> p i c", p=128)

        loads = [
            (up_w[:, :, :], A["up_w"]), (up_h[:, :], A["up_h"]), (dn_h[:, :], A["dn_h"]),
            (dn_w[:, :], A["dn_w"]), (ident[:, :], A["ident"]), (gavg[:, :], A["gavg"]),
            (w1t[:, :], A["W1T"]), (w2t[:, :, :], A["W2T"].rearrange("(f p) c -> p f c", p=128)),
            (g2[:, 0, :, 0:C], A["W1"].rearrange("(f p) c -> p f c", p=128)),
            (b1t[:, :], A["b1"]),
            (coef[:, :, :], A["coef"].rearrange("(f p) k -> p f k", p=128)),
            (b2t[:, :], A["b2"].rearrange("(c o) -> c o", o=1)),
            (win[:, :], A["WinT"]),
            (wo[:, :, :], A["WoT"].rearrange("(t p) e -> p t e", p=C)),
            (nega[:, :, :], A["A_lay"]),
            (dhalf[:, :], A["D"]),
            (av[0:C, 0:2, :], A["sel"].rearrange("p (a b) -> p a b", a=2)),
            (rsel[:, :], A["rsel"]),
            (bu[0:C, 0, :, 0:288].rearrange("p a b -> p a b"), A["conv_w"].partition_broadcast(C)),
            (tapw[C:C + 1, 2, :], A["conv_b"].rearrange("(o d) -> o d", o=1)),
            (wx[:, :, 0:RANK + 2 * DSTATE], A["WxT"].rearrange("(t p) e -> p t e", p=C)),
            (wdt[C:C + 1, :], A["b_dt"].rearrange("(o d) -> o d", o=1)),
            (wdt[32:32 + RANK, :], A["WdtT"]),
        ]
        N_FREE = len(loads) - 3

        PRE = [merged(0, 0, 1), merged(0, 1, 1), merged(1, 1, 1)]
        FULL = merged(1, 1, 1)
        TAIL = [merged(1, 1, 0), merged(1, 0, 0), []]
        SETUP_STEPS = 2
        N_SETUP = 15
        starts = [SETUP_STEPS]
        for m in PRE:
            starts.append(starts[-1] + len(m))
        LOOPS = NS - len(TAIL)
        UF = len(FULL)
        base_full = starts[len(PRE)]
        base_tail = base_full + LOOPS * UF
        assert UF % 2 == 0 and all(len(m) % 2 == 0 for m in PRE + TAIL), [len(m) for m in PRE]

        class Count:

            def __init__(self, multiples, m=1, c=0):
                self.multiples, self.m, self.c = multiples, m, c

            def __add__(self, c):
                if isinstance(c, Count):
                    return Count(self.multiples, self.m + c.m, self.c + c.c)
                return Count(self.multiples, self.m, self.c + c)

            __radd__ = __add__

            def __sub__(self, c):
                return self + -c

            def __mul__(self, m):
                return Count(self.multiples, self.m * m, self.c * m)

            __rmul__ = __mul__

        def val(v):
            return v.multiples[v.m] + v.c if isinstance(v, Count) else v

        class Steps:

            def __init__(self, plan, base, s):
                self.plan, self.base, self.s = plan, base, s
                self.at = {st: i for i, (_, st) in enumerate(plan)}

            def done(self, i):
                return val(self.base + i + 1)

            def freed(self, i):
                return val(self.half(i))

            def freed_all(self, steps):
                last = [max([i for i in steps if i % 2 == p], default=None) for p in range(2)]
                return [(cb_free[p], self.freed(i)) for p, i in enumerate(last) if i is not None]

            def half(self, i):
                if isinstance(self.base, int):
                    return (self.base + i) // 2 + 1
                return self.s * (UF // 2) + (base_full // 2 + i // 2 + 1)


        def run(eng, multiples, lag, unit_fn, step_fn, begin_fn, a_fn, c_fn):
            for it, plan in enumerate(PRE):
                st = Steps(plan, starts[it], it - len(PRE))
                begin_fn(st)
                for i in range(len(plan)):
                    step_fn(st, i)
            for k in range(LEAD):
                for n in range(NU):
                    a_fn(0, k, n)

            def iteration(s, plan, base, first, last):
                st = Steps(plan, base, s)
                begin_fn(st)
                i = 0
                for k in range(NC8):
                    for n in range(NU):
                        unit_fn(s, k, n)
                        if k > 0:
                            c_fn(s, k - 1, n)
                        elif not first:
                            c_fn(s - 1, NC8 - 1, n)
                        ka = k + LEAD
                        if ka < NC8:
                            a_fn(s, ka, n)
                        elif not last:
                            a_fn(s + 1, ka - NC8, n)
                        while i < len(plan) and plan[i][0] + lag <= k * NU + n:
                            step_fn(st, i)
                            i += 1
                for i in range(i, len(plan)):
                    step_fn(st, i)

            iteration(0, FULL, base_full, True, False)
            with eng.Fori(1, LOOPS) as sample:
                s = Count({m: eng.snap(sample * m) if m > 1 else sample for m in multiples})
                iteration(s, FULL, s * UF + base_full, False, False)
            base = base_tail
            for t, plan in enumerate(TAIL):
                iteration(LOOPS + t, plan, base, False, t == len(TAIL) - 1)
                base += len(plan)
            for n in range(NU):
                c_fn(NS - 1, NC8 - 1, n)

        def count(sm, v):
            if isinstance(v, int):
                v = max(v, 0)
            return val(v)

        def stage_sample(st, name):
            return st.s + {"S": 3, "W": 2, "D": 1}[name[0]]

        MULT = {
            "sp": [1, 8, 24, 64, 96, UF // 2, 128, 192, UF, 208, 256],
            "pe": [2, 4, 5, 8, 16, 24, 32, 64, 80, 96, UF // 2, 128, 192, UF],
            "act": [1, 5, 8, 16, 24, 32, 64, UF // 2, 128, 192, UF, 208, 256],
            "dve": [1, 2, 4, 5, 8, 16, 24, 32, 96, 97, UF // 2, 128, 192, UF, 256],
            "pool": [1, 16, 24, 32, UF // 2, 192, UF],
        }

        block = ctx.enter_context(nc.Block())

        @block.sync
        def _(sp):
            for dst, src in loads[:N_FREE]:
                sp.dma_start(dst, src).then_inc(ld_w, 16)
            sp.wait_ge(zset, count(zset, 3))
            sp.sem_inc(sp_passed, 1)
            for dst, src in loads[N_FREE:]:
                sp.dma_start(dst, src).then_inc(ld_w, 16)

            def load_xb(st, b):
                x = stage_sample(st, "S")
                sp.dma_start(xb[:, b % 2], tok(xtok, x, b * T, T)).then_inc(xb_ld[b % 2], 16)

            def load_t1(st, m):
                w = stage_sample(st, "W")
                src = t1_d[bass.ds(val(w), 1)].rearrange("o w f -> (o w f)").rearrange(
                    "(i p c) -> p i c", p=128, c=C)[:, 5 * m:5 * m + 5, :]
                sp.dma_start(t1r[:, m % 2], src).then_inc(t1_ld[m % 2], 16)

            def load_rr(st, m):
                d = stage_sample(st, "D")
                src = v2_d[bass.ds(val(d), 1), 4 * m:4 * m + 4].rearrange("o h w c -> (o h) w c").rearrange(
                    "h w c -> w h c")
                sp.dma_start(rr[:, m % 2], src).then_inc(rr_ld[m % 2], 16)

            def load_xp(st, k):
                d = stage_sample(st, "D")
                sp.dma_start(xp[:, k % 2], tok(xtok, d, k * T, T)).then_inc(xp_ld[k % 2], 16)

            def begin(st):
                if not st.plan:
                    return
                sp.wait_ge(pe_conv, count(pe_conv, st.base))
                sp.sem_inc(sp_passed, 1)
                if ("ST", 0) in st.at:
                    load_xb(st, 0)
                    load_xb(st, 1)
                if ("WG", 0) in st.at:
                    w = stage_sample(st, "W")
                    for p in range(2):
                        sp.wait_ge(t1_st[p], count(t1_st[p], (w + 1) * 64))
                        sp.sem_inc(sp_passed, 1)
                    load_t1(st, 0)
                    load_t1(st, 1)
                if ("DG", 0) in st.at:
                    d = stage_sample(st, "D")
                    sp.wait_ge(v2_st[0], count(v2_st[0], (d + 1) * (16 * 13)))
                    sp.sem_inc(sp_passed, 1)
                    sp.wait_ge(v2_st[1], count(v2_st[1], (d + 1) * (16 * 12)))
                    sp.sem_inc(sp_passed, 1)
                    for m in range(2):
                        load_rr(st, m)
                        load_xp(st, m)

            def step(st, i):
                name, b = st.plan[i][1][:2]
                if name == "SB":
                    x = stage_sample(st, "S")
                    for bank_free, n_free in st.freed_all([i, st.at[("SA", b)]]):
                        sp.wait_ge(bank_free, n_free)
                        sp.sem_inc(sp_passed, 1)
                    dst = t1_d[bass.ds(val(x), 1), :, b * XB_H * C:(b + 1) * XB_H * C].rearrange(
                        "o w f -> (o w) f")
                    sp.dma_start(dst, t1s[:, b % 2].rearrange("p h c -> p (h c)"))\
                        .then_inc(t1_st[b % 2], 16)
                    if b + 2 < HH // XB_H:
                        sp.wait_ge(pe_conv, st.done(i))
                        sp.sem_inc(sp_passed, 1)
                        load_xb(st, b + 2)
                if name == "W_up":
                    for m in range(10):
                        if (5 * m + 4) // 2 == b and m + 2 < 10:
                            sp.wait_ge(pe_conv, st.done(i))
                            sp.sem_inc(sp_passed, 1)
                            load_t1(st, m + 2)
                if name == "W_dn":
                    w = stage_sample(st, "W")
                    sp.wait_ge(cb_free[(i) % 2], st.freed(i))
                    sp.sem_inc(sp_passed, 1)
                    dst = v2_d[bass.ds(val(w), 1), :, 4 * b:4 * b + 4, :].rearrange("o h w c -> (o h) (w c)")
                    sp.dma_start(dst, v2s[:, b % 2]).then_inc(v2_st[b % 2], 16)
                if name == "D_xt" and b + 2 < NC8:
                    sp.wait_ge(pe_conv, st.done(i))
                    sp.sem_inc(sp_passed, 1)
                    load_xp(st, b + 2)
                if name in ("D_lo", "D_hi"):
                    m = 2 * b + (name == "D_hi")
                    if m + 2 < 2 * NC8:
                        sp.wait_ge(pe_conv, st.done(i))
                        sp.sem_inc(sp_passed, 1)
                        load_rr(st, m + 2)
                if name == "D_hi":
                    d = stage_sample(st, "D")
                    for bank_free, n_free in st.freed_all([i, st.at[("D_lo", b)]]):
                        sp.wait_ge(bank_free, n_free)
                        sp.sem_inc(sp_passed, 1)
                    dst = x1_d[bass.ds(val(d), 1), :, b * T:(b + 1) * T].rearrange("o c t -> (o c) t")
                    sp.dma_start(dst, x1s[:, b % 2]).then_inc(x1_st[b % 2], 16)

            def load_x1c(s, k):
                for p in range(2):
                    sp.wait_ge(x1_st[p], count(x1_st[p], (s + 1) * 64))
                    sp.sem_inc(sp_passed, 1)
                sp.wait_ge(pe_out, count(pe_out, s * NC8 + k - 3))
                sp.sem_inc(sp_passed, 1)
                src = x1_d[bass.ds(val(s), 1), :, k * T:(k + 1) * T].rearrange("o c t -> (o c) t")
                sp.dma_start(x1c[:, k % 4], src).then_inc(x1c_ld[k % 4], 16)

            def a_part(s, k, n):
                G = s * NC8 + k
                if n == 0 and isinstance(G, int) and G == 0:
                    load_x1c(s, k)
                if n == 14 and not (isinstance(G, int) and G + 1 == NS * NC8):
                    load_x1c(s + (k + 1) // NC8, (k + 1) % NC8)
                if n == 22:
                    sp.wait_ge(dve_sp, count(dve_sp, G * 3 + 2))
                    sp.sem_inc(sp_passed, 1)
                    for ld in (rd_ld, ru_ld):
                        sp.wait_ge(ld[k % 2], count(ld[k % 2], s * (4 * 64) + (k // 2) * 64))
                        sp.sem_inc(sp_passed, 1)
                    sp.dma_start(dl_d[k % 2].rearrange("(t p) f -> p t f", p=C), t0[:, :, :])\
                        .then_inc(dl_st, 16)
                    sp.wait_ge(dve_sp, count(dve_sp, G * 3 + 3))
                    sp.sem_inc(sp_passed, 1)
                    sp.dma_start(du_d[k % 2].rearrange("(t p) f -> p t f", p=C), t1[:, :, :])\
                        .then_inc(du_st, 16)

            def spread(s, k):
                G = s * NC8 + k
                sp.wait_ge(dl_st, count(dl_st, (G + 1) * 16))
                sp.sem_inc(sp_passed, 1)
                sp.wait_ge(act_a, count(act_a, (G - 1) * NU))
                sp.sem_inc(sp_passed, 1)
                for r in range(4):
                    sp.dma_start(rep_d[32 * r:32 * r + 32, k % 2],
                                 dl_d[k % 2].rearrange("(j p) f -> p j f", p=32))\
                        .then_inc(rd_ld[k % 2], 16)
                sp.wait_ge(du_st, count(du_st, (G + 1) * 16))
                sp.sem_inc(sp_passed, 1)
                sp.wait_ge(dve_bu, count(dve_bu, (G - 1) * (NU // 2)))
                sp.sem_inc(sp_passed, 1)
                for r in range(4):
                    sp.dma_start(rep_u[32 * r:32 * r + 32, k % 2],
                                 du_d[k % 2].rearrange("(j p) f -> p j f", p=32))\
                        .then_inc(ru_ld[k % 2], 16)

            def a_with_spread(s, k, n):
                a_part(s, k, n)
                if n == 23:
                    spread(s, k)

            def c_part(s, k, n):
                if n != 12:
                    return
                G = s * NC8 + k
                sp.wait_ge(act_out, count(act_out, G + 1))
                sp.sem_inc(sp_passed, 1)
                sp.dma_start(tok(otok, s, k * T, T), os_[:, k % 2]).then_inc(out_st[k % 2], 16)

            run(nc.sync, MULT["sp"], 1, lambda s, k, n: None, step, begin, a_with_spread, c_part)
            for p in range(2):
                sp.wait_ge(out_st[p], count(out_st[p], NS * NC8 // 2 * 16))
                sp.sem_inc(sp_passed, 1)
                sp.wait_ge(rd_ld[p], count(rd_ld[p], NS * NC8 // 2 * 64))
                sp.sem_inc(sp_passed, 1)
                sp.wait_ge(ru_ld[p], count(ru_ld[p], NS * NC8 // 2 * 64))
                sp.sem_inc(sp_passed, 1)

        @block.tensor
        def _(pe):
            pe.wait_ge(ld_w, count(ld_w, 16 * len(loads)))
            pe.wait_ge(setup_v, count(setup_v, 5))
            for f in range(NF):
                mm = pe.matmul(cb[0:C, 0, 0:C], g2[:, 0, f, 0:C], g2[:, 1, f, 0:C], start=(f == 0), stop=(f == NF - 1))
            mm.then_inc(pe_conv, 1)
            for f in range(NF):
                mm = pe.matmul(cb[0:C, 1, 0:1], w2t[:, f, :], fcst[:, f:f + 1], start=(f == 0), stop=(f == NF - 1))
            mm.then_inc(pe_conv, 1)
            pe.wait_ge(setup_v, count(setup_v, N_SETUP))
            pe.wait_ge(setup_a, count(setup_a, 3))

            def step(st, i):
                name, b = st.plan[i][1][:2]
                bank = cb[:, i % 2]
                x = stage_sample(st, name)
                at = st.at
                made = {"W_f": [("W_up", b), ("WG", 0)], "W_2": [("W_f", b, f) for f in range(NF)],
                        "W_dn": [("W_2", b)], "D_lo": [("D_xt", b)], "D_hi": [("D_xt", b)]}.get(name, [])
                for bank_free, n_free in st.freed_all([i - 2] + [at[m] for m in made]):
                    pe.wait_ge(bank_free, n_free)
                if name == "ST":
                    pe.wait_ge(xb_ld[b % 2], count(xb_ld[b % 2], x * 64 + (b // 2 + 1) * 16))
                    for j in range(4):
                        mm = pe.transpose(bank[0:C, 128 * j:128 * j + 128], xb[:, b % 2, j, :], ident[:, :])
                elif name in ("SA", "SB"):
                    mm = pe.matmul(bank[0:GW, 0:4 * C], up_w[:, int(name == "SB"), :],
                                   xb[:, b % 2].rearrange("p i c -> p (i c)"), start=True, stop=True)
                elif name in ("SG1", "DG1"):
                    v = int(name == "DG1")
                    pe.wait_ge(dve_d if v else dve_s, count(dve_d if v else dve_s, x * (5 if v else 4) + 1 + v))
                    mm = pe.matmul(bank[0:C, 0:1], gavg[:, :], mv[:, v, 0:1], start=True, stop=True)
                elif name in ("SG2", "DG2"):
                    v = int(name == "DG2")
                    pe.wait_ge(dve_d if v else dve_s, count(dve_d if v else dve_s, x * (5 if v else 4) + 3 + v))
                    mm = pe.matmul(bank[0:C, 0:1], gavg[:, :], vv[:, v:v + 1], start=True, stop=True)
                elif name == "WG":
                    pe.wait_ge(dve_s, count(dve_s, x * 4 + 4))
                    for f in range(NF):
                        mm = pe.matmul(bank[:, f:f + 1], w1t[:, 128 * f:128 * f + 128], gnx[:, 1:2],
                                       start=True, stop=True)
                elif name == "W_up":
                    for e in range(2):
                        i2 = 2 * b + e
                        m = i2 // 5
                        if i2 % 5 == 0 or e == 0:
                            pe.wait_ge(t1_ld[m % 2], count(t1_ld[m % 2], x * 80 + (m // 2 + 1) * 16))
                        mm = pe.matmul(bank[0:C, e * 2 * GH:(e + 1) * 2 * GH], t1r[:, m % 2, i2 % 5, :],
                                       up_h[:, :], start=True, stop=True)
                elif name == "W_f":
                    f = st.plan[i][1][2]
                    if f == 0:
                        pe.wait_ge(dve_w, count(dve_w, x * 2 + 2))
                    mm = pe.matmul(bank[:, 0:BC], w1a[:, 128 * f:128 * f + 128], xu[:, b % 2, :],
                                   start=True, stop=True)
                elif name == "W_2":
                    for j in range(4):
                        for f in range(NF):
                            mm = pe.matmul(bank[0:GH, C * j:C * j + C], g2[:, b % 2, f, GH * j:GH * j + GH],
                                           w2c[:, f, :], start=(f == 0), stop=(f == NF - 1))
                elif name == "W_dn":
                    mm = pe.matmul(bank[0:HH, 0:4 * C], dn_h[:, :], vr[:, b % 2, :], start=True, stop=True)
                elif name == "DG":
                    pe.wait_ge(dve_d, count(dve_d, x * 5 + 1))
                    mm = pe.matmul(bank[0:C, 0:1], wlin[:, :], gnd[:, 1:2], start=True, stop=True)
                elif name == "D_xt":
                    pe.wait_ge(xp_ld[b % 2], count(xp_ld[b % 2], x * 64 + (b // 2 + 1) * 16))
                    for j in range(4):
                        mm = pe.transpose(bank[0:C, 128 * j:128 * j + 128], xp[:, b % 2, j, :], ident[:, :])
                elif name in ("D_lo", "D_hi"):
                    hf = int(name == "D_hi")
                    m = 2 * b + hf
                    pe.wait_ge(rr_ld[m % 2], count(rr_ld[m % 2], x * 128 + (m // 2 + 1) * 16))
                    o = bank[0:C, 0:4 * 96].rearrange("c (h w) -> c h w", h=4)
                    pe.matmul(o[:, :, 0:WW], wtot[:, :],
                              xt[:, b % 2, hf * 256:hf * 256 + 256].rearrange("c (h w) -> c h w", h=4),
                              start=True, stop=False, skip_group_check=True)
                    for j in range(4):
                        mm = pe.matmul(o[:, j, :], rr[:, m % 2, j, :], dn_w[:, :], start=False, stop=(j == 3),
                                       skip_group_check=True)
                elif name in ("DPAD", "WPAD"):
                    mm = pe.transpose(bank[0:C, 0:C], ident[0:C, 0:C], ident[0:C, 0:C])
                mm.then_inc(pe_conv, 1)

            def unit(s, k, n):
                G = s * NC8 + k
                q, j = n // NJ, n % NJ
                if isinstance(G, int) and G == 0 and n == 0:
                    spread_bc(G, k, 0)
                if j == 4:
                    if q + 1 < NQ:
                        spread_bc(G, k, q + 1)
                    elif not (isinstance(G, int) and G + 1 == NS * NC8):
                        spread_bc(G + 1, (k + 1) % NC8, 0)
                for r in range(summed(n - 1), summed(n)):
                    reduce(s, k, r)
                if n == 6:
                    zproj(s, k)

            def summed(n):
                return max(0, min(n - 2, 2 * (n - 5) + 1))

            def spread_bc(G, k, q):
                if q == 0:
                    pe.wait_ge(dve_bc, count(dve_bc, G * 2 + 2))
                    pe.wait_ge(act_dbc, count(act_dbc, after_dbc(G + 1)))
                pe.wait_ge(dve_bu, count(dve_bu, G * (NU // 2) + 3 * q))
                pe.matmul(pb[:, :], selb[:, q, :], bc3[:, k % 4, :], start=True, stop=True).then_inc(pe_b, 1)
                pe.wait_ge(act_c, count(act_c, G * NQ + q))
                if q == 2:
                    pe.wait_ge(act_out, count(act_out, G))
                if q == 3:
                    pe.wait_ge(act_dbc, count(act_dbc, after_dbc(G + 2)))
                pe.matmul(pm[:, :], selb[:, NQ + q, :], bc3[:, k % 4, :], start=True, stop=True).then_inc(pe_c, 1)

            def after_dbc(G):
                return NS * NC8 * 3 if isinstance(G, int) and G >= NS * NC8 else G * 3 + 2

            def reduce(s, k, n):
                G = s * NC8 + k
                q, j = n // NJ, n % NJ
                if n in (0, 3):
                    pe.wait_ge(dve_y, count(dve_y, (G - 1) * 3 + 1 + n // 3))
                pe.wait_ge(pool_hc, count(pool_hc, G * NU + n + 1))
                pe.matmul(py[32 * (j % 3):32 * (j % 3) + 32, j // 3, :], rsel[:, :], hc[:, n % 4, :],
                          start=(q == 0), stop=(q == NQ - 1)).then_inc(pe_red, 1)

            def zproj(s, k):
                G = s * NC8 + k
                tail = isinstance(G, int) and G + 3 > NS * NC8
                pe.wait_ge(dve_xcs, count(dve_xcs, NS * NC8 if tail else G + 3))
                pe.wait_ge(dve_sp, count(dve_sp, NS * NC8 * 3 if tail else (G + 2) * 3))
                for t in range(2):
                    mm = pe.matmul(px[0:C, t, :], win[:, DI + C * t:DI + C * t + C], xn[0:C, k % 4, 2:T + 2],
                                   start=True, stop=True)
                mm.then_inc(pe_z, 1)

            def a_part(s, k, n):
                G = s * NC8 + k
                if n == 1:
                    pe.wait_ge(act_xn, count(act_xn, G + 1))
                    pe.wait_ge(dve_sp, count(dve_sp, G * 3))
                    pe.wait_ge(dve_zs, count(dve_zs, G - 2))
                    for t in range(2):
                        d = slice(C * t, C * t + C)
                        pe.matmul(px[0:C, t, :], tapw[0:C + 1, 2, d], xn[0:C + 1, k % 4, 2:T + 2], start=True, stop=False)
                        pe.matmul(px[0:C, t, :], tapw[0:C, 1, d], xn[0:C, k % 4, 1:T + 1], start=False, stop=False)
                        mm = pe.matmul(px[0:C, t, :], tapw[0:C, 0, d], xn[0:C, k % 4, 0:T], start=False, stop=True)
                    mm.then_inc(pe_x, 1)
                if n == 13:
                    pe.wait_ge(dve_xcs, count(dve_xcs, G + 1))
                    pe.wait_ge(act_dbc, count(act_dbc, G * 3))
                    pe.wait_ge(act_c, count(act_c, (G - 2) * NQ + 3))
                    for t in range(2):
                        mm = pe.matmul(pm[0:C, :], wx[:, t, :], xcs[:, k % 4, t, :], start=(t == 0), stop=(t == 1))
                    mm.then_inc(pe_dbc, 1)
                if n == 15:
                    pe.wait_ge(act_dbc, count(act_dbc, G * 3 + 1))
                    pe.wait_ge(dve_zs, count(dve_zs, G - 1))
                    for t in range(2):
                        mm = pe.matmul(px[0:C, t, :], wdt[:, C * t:C * t + C], dbc[:, :], start=True, stop=True)
                    mm.then_inc(pe_dt, 1)

            def c_part(s, k, n):
                G = s * NC8 + k
                if n == 0:
                    for r in range(summed(NU - 1), NU):
                        reduce(s, k, r)
                if n != 8:
                    return
                pe.wait_ge(dve_y, count(dve_y, G * 3 + 3))
                pe.wait_ge(act_c, count(act_c, NS * NC8 * NQ if isinstance(G, int) and G + 1 == NS * NC8
                                        else (G + 1) * NQ + 2))
                for b in range(4):
                    tb = slice(128 * b, 128 * b + 128)
                    o = pm[:, C * b:C * b + C]
                    for t in range(2):
                        pe.matmul(o, yy[:, t, tb], wo[:, t, :], start=(t == 0), stop=False)
                    mm = pe.matmul(o, x1c[:, k % 4, tb], ident[0:C, 0:C], start=False, stop=True)
                mm.then_inc(pe_out, 1)

            run(nc.tensor, MULT["pe"], 0, unit, step, lambda st: None, a_part, c_part)

        @block.scalar
        def _(act):
            act.wait_ge(ld_w, count(ld_w, 16 * len(loads)))
            act.activation(selb[:, 0:NQ, :].rearrange("p q m -> p (q m)"), av[0:C, 0, :], ACT.Copy).then_inc(setup_a, 1)
            act.activation(selb[:, NQ:2 * NQ, :].rearrange("p q m -> p (q m)"), av[0:C, 1, :], ACT.Copy).then_inc(setup_a, 1)
            act.activation(nega[:, :, :], nega[:, :, :], ACT.Exp).then_inc(setup_a, 1)
            act.wait_ge(setup_v, count(setup_v, N_SETUP))

            def step(st, i):
                key = st.plan[i][1]
                name, b = key[:2]
                bank = cb[:, i % 2]
                x = stage_sample(st, name)
                out = None
                if name in ("SA", "SB"):
                    par = int(name == "SB")
                    if par == 0:
                        act.wait_ge(t1_st[b % 2], count(t1_st[b % 2], x * 64 + (b // 2) * 16))
                    out = t1s[:, b % 2].rearrange("p (i r) c -> p i r c", r=2)[:, :, par, :]
                    src = bank[0:GW, 0:4 * C].rearrange("p (i c) -> p i c", i=4)
                elif name == "W_up":
                    out, src = xu[:, b % 2, :], bank[0:C, 0:BC]
                elif name == "W_dn":
                    act.wait_ge(v2_st[b % 2], count(v2_st[b % 2], x * (16 * (13 - b % 2)) + (b // 2) * 16))
                    out, src = v2s[:, b % 2, :], bank[0:HH, 0:4 * C]
                if out is not None:
                    act.wait_ge(pe_conv, st.done(i))
                    act.activation(out, src, ACT.Copy).then_inc(cb_free[i % 2], 1)
                elif name == "W_f":
                    f = key[2]
                    act.wait_ge(pe_conv, st.done(i))
                    if b == 0 and f == 0:
                        act.wait_ge(cb_free[(st.at[("WG", 0)]) % 2], st.freed(st.at[("WG", 0)]))
                    act.activation(g2[:, b % 2, f, :], bank[:, 0:BC], ACT.Square, bias=b1a[:, f:f + 1])\
                        .then_inc(cb_free[i % 2], 1)
                elif name in ("D_lo", "D_hi"):
                    hf = int(name == "D_hi")
                    act.wait_ge(pe_conv, st.done(i))
                    if b == 0:
                        act.wait_ge(cb_free[(st.at[("DG", 0)]) % 2], st.freed(st.at[("DG", 0)]))
                    act.wait_ge(x1_st[b % 2], count(x1_st[b % 2], x * 64 + (b // 2) * 16))
                    act.wait_ge(x1_bn, count(x1_bn, x * 8 + b - 1))
                    act.activation(x1s[:, b % 2, 256 * hf:256 * hf + 256].rearrange("c (h w) -> c h w", h=4),
                                   bank[0:C, 0:384].rearrange("c (h w) -> c h w", h=4)[:, :, 0:WW],
                                   ACT.Identity, bias=cst[:, 0:1]).then_inc(cb_free[i % 2], 1)

            def unit(s, k, n):
                G = s * NC8 + k
                q, j = n // NJ, n % NJ
                if n == 0:
                    act.wait_ge(rd_ld[k % 2], count(rd_ld[k % 2], s * (4 * 64) + (k // 2 + 1) * 64))
                act.wait_ge(dve_h, count(dve_h, G * NU + n - 3))
                act.activation(av[:, n % 4, :], rep_d[:, k % 2, j, :], ACT.Exp, scale=nega[:, q, j:j + 1])\
                    .then_inc(act_a, 1)
                if j == 1:
                    act.wait_ge(pe_c, count(pe_c, G * NQ + q + 1))
                    act.wait_ge(pool_hc, count(pool_hc, G * NU + NJ * (q - 1)))
                    act.activation(cs[:, q % 2, :], pm[:, :], ACT.Copy).then_inc(act_c, 1)
                if n == 9:
                    act.wait_ge(pe_z, count(pe_z, G + 1))
                    act.wait_ge(dve_xcs, count(dve_xcs, G + 3 if not (isinstance(G, int) and G + 3 > NS * NC8) else NS * NC8))
                    act.activation(t2[:, :, :], px[0:C, :, :], ACT.Tanh, scale=0.5).then_inc(act_tz, 1)

            def a_part(s, k, n):
                G = s * NC8 + k
                if n == 0:
                    if k == 0:
                        act.wait_ge(dve_d, count(dve_d, s * 5 + 5))
                        act.wait_ge(pool_d, count(pool_d, s + 1))
                        act.activation(gna[:, :], gn1[:, :], ACT.Copy).then_inc(act_gn, 1)
                        act.wait_ge(act_gn, count(act_gn, s + 1))
                        act.wait_ge(pe_z, count(pe_z, G - 2))
                        act.activation(xn[0:C, 0, 0:2], zero2[:, :], ACT.Copy).then_inc(act_halo, 1)
                    else:
                        act.wait_ge(act_xn, count(act_xn, G))
                        act.wait_ge(pe_z, count(pe_z, G - 2))
                        act.activation(xn[0:C, k % 4, 0:2], xn[0:C, (k - 1) % 4, T:T + 2], ACT.Copy).then_inc(act_halo, 1)
                    act.wait_ge(x1c_ld[k % 4], count(x1c_ld[k % 4], s * 32 + (k // 4 + 1) * 16))
                    act.wait_ge(act_halo, count(act_halo, G + 1))
                    act.activation(xn[0:C, k % 4, 2:T + 2], x1c[:, k % 4, :], ACT.Identity,
                                   bias=gna[:, 1:2], scale=gna[:, 0:1]).then_inc(act_xn, 1)
                if n == 4:
                    act.wait_ge(pe_x, count(pe_x, G + 1))
                    act.wait_ge(dve_sp, count(dve_sp, G * 3))
                    act.wait_ge(dve_zs, count(dve_zs, G - 2))
                    act.activation(t2[:, :, :], px[0:C, :, :], ACT.Tanh, scale=0.5).then_inc(act_tx, 1)
                if n == 16:
                    act.wait_ge(pe_dbc, count(pe_dbc, G + 1))
                    act.wait_ge(pe_dt, count(pe_dt, G))
                    act.wait_ge(dve_bc, count(dve_bc, G * 2))
                    act.activation(dbc[0:C, :], pm[0:C, :], ACT.Copy).then_inc(act_dbc, 1)
                    act.wait_ge(pe_c, count(pe_c, (G - 2) * NQ))
                    act.activation(bc3[0:32, k % 4, :], pm[0:32, :], ACT.Copy).then_inc(act_dbc, 1)
                if n == 18:
                    act.wait_ge(dve_bc, count(dve_bc, G * 2 + 1))
                    act.activation(bc3[32:64, k % 4, :], t1[32:64, 0, :], ACT.Copy).then_inc(act_dbc, 1)
                if n == 19:
                    act.wait_ge(pe_dt, count(pe_dt, G + 1))
                    act.wait_ge(dl_st, count(dl_st, G * 16))
                    act.wait_ge(du_st, count(du_st, G * 16))
                    act.activation(t0[:, :, :], px[0:C, :, :], ACT.Abs).then_inc(act_sp, 1)
                    act.wait_ge(act_sp, count(act_sp, G * 3 + 1))
                    act.wait_ge(dve_bc, count(dve_bc, G * 2 + 2))
                    act.activation(t1[:, :, :], t0[:, :, :], ACT.Exp, scale=-1.0).then_inc(act_sp, 1)
                    act.wait_ge(act_sp, count(act_sp, G * 3 + 2))
                    act.activation(t0[:, :, :], t1[:, :, :], ACT.Ln, bias=1.0).then_inc(act_sp, 1)

            def c_part(s, k, n):
                if n != 11:
                    return
                G = s * NC8 + k
                act.wait_ge(pe_out, count(pe_out, G + 1))
                act.wait_ge(out_st[k % 2], count(out_st[k % 2], s * 64 + (k // 2) * 16))
                act.activation(os_[:, k % 2].rearrange("p b c -> p (b c)"), pm[:, 0:4 * C], ACT.Copy).then_inc(act_out, 1)

            run(nc.scalar, MULT["act"], 3, unit, step, lambda st: None, a_part, c_part)

        @block.vector
        def _(dve):
            dve.memset(wx[:, :, :], 0.0).then_inc(zset, 1)
            dve.memset(wdt[:, :], 0.0).then_inc(zset, 1)
            dve.memset(xn[C:C + 1, :, :], 1.0)
            dve.memset(dbc[C:C + 1, :], 1.0)
            dve.memset(mhalf[:, :], -0.5)
            dve.memset(zero2[:, :], 0.0).then_inc(zset, 1)
            dve.wait_ge(ld_w, count(ld_w, 16 * len(loads)))
            n_set = [0]

            def setup(ins):
                n_set[0] += 1
                ins.then_inc(setup_v, 1)
                dve.wait_ge(setup_v, count(setup_v, n_set[0]))

            for f in range(NF):
                setup(dve.tensor_scalar(g2[:, 1, f, 0:C], w2t[:, f, :], coef[:, f, 1:2], None, ALU.mult))
            setup(dve.tensor_tensor(fcst[:, :], b1t[:, :], coef[:, :, 1], ALU.mult))
            setup(dve.tensor_tensor(fcst[:, :], fcst[:, :], coef[:, :, 0], ALU.add))
            for f in range(NF):
                setup(dve.tensor_scalar(w2c[:, f, :], w2t[:, f, :], coef[:, f, 2:3], None, ALU.mult))
            for t in range(3):
                setup(dve.tensor_tensor(tapw[0:C, t, :].rearrange("p (a b) -> p a b", a=2),
                                        win[:, 0:DI].rearrange("p (a b) -> p a b", a=2),
                                        bu[0:C, 0, :, t:288:3], ALU.mult))
            setup(dve.tensor_scalar(wx[:, :, :], wx[:, :, :], 0.5, None, ALU.mult))
            setup(dve.tensor_scalar(wo[:, :, :], wo[:, :, :], 0.5, None, ALU.mult))
            setup(dve.tensor_scalar(dhalf[:, :], dhalf[:, :], 0.5, None, ALU.mult))
            dve.wait_ge(setup_a, count(setup_a, 3))
            setup(dve.tensor_scalar(nega[:, :, :], nega[:, :, :], -1.0, None, ALU.mult))
            dve.wait_ge(pe_conv, count(pe_conv, 2))
            dve.tensor_copy(wlin[:, :], cb[0:C, 0, 0:C]).then_inc(cb_free[0], 1)
            dve.tensor_tensor(cbase[:, :], cb[0:C, 1, 0:1], b2t[:, :], ALU.add).then_inc(cb_free[1], 1)
            assert n_set[0] == N_SETUP

            def step(st, i):
                name, b = st.plan[i][1][:2]
                bank = cb[:, i % 2]
                x = stage_sample(st, name)
                fr = cb_free[i % 2]
                if name == "ST":
                    dve.wait_ge(pe_conv, st.done(i))
                    dve.bn_stats(bst[:, 0, b, :], bank[0:C, :]).then_inc(fr, 1)
                    if b == 7:
                        for bank_free, n_free in st.freed_all([i, i - 1]):
                            dve.wait_ge(bank_free, n_free)
                        dve.memset(dm[:, 0:1], 0.0)
                        dve.bn_aggr(mv[:, 0, :], bst[:, 0].rearrange("c a b -> c (a b)")).then_inc(dve_s, 1)
                elif name in ("SG1", "DG1"):
                    v = int(name == "DG1")
                    sm, c0 = (dve_d, x * 5 + 1) if v else (dve_s, x * 4)
                    dve.wait_ge(pe_conv, st.done(i))
                    dve.tensor_copy(mg[:, v:v + 1], bank[0:C, 0:1]).then_inc(fr, 1)
                    dve.wait_ge(cb_free[(i) % 2], st.freed(i))
                    dve.tensor_tensor(dm[:, v:v + 1], mv[:, v, 0:1], mg[:, v:v + 1], ALU.subtract).then_inc(sm, 1)
                    dve.wait_ge(sm, count(sm, c0 + 2))
                    dve.scalar_tensor_tensor(out=vv[:, v:v + 1], in0=dm[:, v:v + 1], scalar=dm[:, v:v + 1],
                                             in1=mv[:, v, 1:2], op0=ALU.mult, op1=ALU.add).then_inc(sm, 1)
                elif name in ("SG2", "DG2"):
                    v = int(name == "DG2")
                    sm, c0, pl, gn = (dve_d, x * 5 + 1, pool_d, gn1) if v else (dve_s, x * 4, pool_s, gnx)
                    dve.wait_ge(pe_conv, st.done(i))
                    dve.tensor_scalar(ve[:, v:v + 1], bank[0:C, 0:1], 1e-5, None, ALU.add).then_inc(fr, 1)
                    dve.wait_ge(pl, count(pl, x + 1))
                    dve.scalar_tensor_tensor(out=gn[:, 1:2], in0=mg[:, v:v + 1], scalar=-1.0, in1=gn[:, 0:1],
                                             op0=ALU.mult, op1=ALU.mult).then_inc(sm, 1)
                elif name == "WG":
                    dve.wait_ge(dve_s, count(dve_s, x * 4 + 4))
                    dve.wait_ge(cb_free[(i - 1) % 2], st.freed(i - 1))
                    dve.wait_ge(cb_free[(i - 2) % 2], st.freed(i - 2))
                    dve.tensor_scalar(w1a[:, :], w1t[:, :], gnx[:, 0:1], None, ALU.mult).then_inc(dve_w, 1)
                    dve.tensor_copy(gnd[:, :], gnx[:, :]).then_inc(dve_w, 1)
                    dve.wait_ge(pe_conv, st.done(i))
                    dve.tensor_tensor(b1a[:, :], bank[:, 0:NF], b1t[:, :], ALU.add).then_inc(fr, 1)
                elif name == "W_2":
                    dve.wait_ge(pe_conv, st.done(i))
                    dve.tensor_copy(vr[:, b % 2, :], bank[0:GH, 0:4 * C]).then_inc(fr, 1)
                elif name == "DG":
                    dve.wait_ge(dve_w, count(dve_w, x * 2 + 2))
                    dve.wait_ge(cb_free[(i - 1) % 2], st.freed(i - 1))
                    dve.wait_ge(cb_free[(i - 2) % 2], st.freed(i - 2))
                    dve.scalar_tensor_tensor(out=wtot[:, :], in0=wlin[:, :], scalar=gnd[:, 0:1], in1=ident[0:C, 0:C],
                                             op0=ALU.mult, op1=ALU.add).then_inc(dve_d, 1)
                    dve.wait_ge(pe_conv, st.done(i))
                    dve.tensor_tensor(cst[:, :], bank[0:C, 0:1], cbase[:, :], ALU.add).then_inc(fr, 1)
                elif name == "D_xt":
                    dve.wait_ge(pe_conv, st.done(i))
                    dve.tensor_copy(xt[:, b % 2, :], bank[0:C, :]).then_inc(fr, 1)
                elif name == "D_hi":
                    for bank_free, n_free in st.freed_all([i, st.at[("D_lo", b)]]):
                        dve.wait_ge(bank_free, n_free)
                    dve.bn_stats(bst[:, 1, b, :], x1s[:, b % 2, :]).then_inc(x1_bn, 1)
                    if b == 7:
                        dve.wait_ge(x1_bn, count(x1_bn, x * 8 + 8))
                        dve.memset(dm[:, 1:2], 0.0)
                        dve.bn_aggr(mv[:, 1, :], bst[:, 1].rearrange("c a b -> c (a b)")).then_inc(dve_d, 1)
                elif name in ("DPAD", "WPAD"):
                    dve.wait_ge(pe_conv, st.done(i))
                    dve.tensor_copy(dm[:, 1:2], bank[0:C, 0:1]).then_inc(fr, 1)

            def product(s, k, m):
                G = s * NC8 + k
                q, j = 2 * m // NJ, 2 * m % NJ
                if m == 0:
                    dve.wait_ge(ru_ld[k % 2], count(ru_ld[k % 2], s * (4 * 64) + (k // 2 + 1) * 64))
                if j == 0:
                    dve.wait_ge(pe_b, count(pe_b, G * NQ + q + 1))
                dve.wait_ge(pool_hc, count(pool_hc, G * NU + 2 * (m - 3)))
                dve.tensor_tensor(bu[:, m % 4], rep_u[:, k % 2, j:j + 2, :],
                                  pb[:, None, :].broadcast_to([128, 2, T]), ALU.mult).then_inc(dve_bu, 1)

            def unit(s, k, n):
                G = s * NC8 + k
                q, j = n // NJ, n % NJ
                m = n // 2
                if n == 0:
                    if k == 0:
                        dve.wait_ge(dve_stt, count(dve_stt, G * (NU // 2) + s))
                        dve.wait_ge(dve_h, count(dve_h, G * NU))
                        dve.memset(state[:, :, :], 0.0).then_inc(dve_stt, 1)
                    product(s, k, 0)
                if n % 2 == 0 and m + 1 < NU // 2:
                    product(s, k, m + 1)
                dve.wait_ge(act_a, count(act_a, G * NU + n + 1))
                if n == 0:
                    dve.wait_ge(dve_stt, count(dve_stt, G * (NU // 2) + s + 1))
                if n % 2 == 0:
                    dve.wait_ge(dve_bu, count(dve_bu, G * (NU // 2) + m + 1))
                h = bu[:, m % 4, n % 2, :]
                dve.tensor_tensor_scan(h, av[:, n % 4, :], h, state[:, q, j:j + 1], ALU.mult, ALU.add)\
                    .then_inc(dve_h, 1)
                if n % 2 == 1:
                    dve.wait_ge(dve_h, count(dve_h, G * NU + n + 1))
                    dve.tensor_copy(state[:, q, j - 1:j + 1], bu[:, m % 4, :, T - 1]).then_inc(dve_stt, 1)
                if n == 9:
                    dve.wait_ge(act_tz, count(act_tz, G + 1))
                    dve.scalar_tensor_tensor(out=zs[:, :, :], in0=t2[:, :, :], scalar=1.0, in1=px[0:C, :, :],
                                             op0=ALU.add, op1=ALU.mult).then_inc(dve_zs, 1)

            def a_part(s, k, n):
                G = s * NC8 + k
                if n == 5:
                    dve.wait_ge(act_tx, count(act_tx, G + 1))
                    dve.scalar_tensor_tensor(out=xcs[:, k % 4], in0=t2[:, :, :], scalar=1.0, in1=px[0:C, :, :],
                                             op0=ALU.add, op1=ALU.mult).then_inc(dve_xcs, 1)
                if n == 15:
                    dve.wait_ge(act_dbc, count(act_dbc, G * 3 + 2))
                    dve.wait_ge(du_st, count(du_st, G * 16))
                    dve.tensor_tensor(t1[32:64, 0, :], dbc[0:32, :], bc3[0:32, k % 4, :], ALU.subtract)\
                        .then_inc(dve_bc, 1)
                if n == 17:
                    dve.wait_ge(act_dbc, count(act_dbc, G * 3 + 3))
                    dve.tensor_tensor(bc3[64:96, k % 4, :], t1[32:64, 0, :], bc3[32:64, k % 4, :], ALU.subtract)\
                        .then_inc(dve_bc, 1)
                if n == 18:
                    dve.wait_ge(act_sp, count(act_sp, G * 3 + 2))
                    dve.wait_ge(dve_zs, count(dve_zs, G - 1))
                    dve.tensor_scalar(t2[:, :, :], t1[:, :, :], 1.0, 1.0, ALU.add, ALU.subtract).then_inc(dve_sp, 1)
                if n == 22:
                    dve.wait_ge(pool_sp, count(pool_sp, G * 2 + 2))
                    dve.scalar_tensor_tensor(out=t0[:, :, :], in0=px[0:C, :, :], scalar=0.0, in1=t2[:, :, :],
                                             op0=ALU.max, op1=ALU.add).then_inc(dve_sp, 1)
                    dve.wait_ge(dve_sp, count(dve_sp, G * 3 + 2))
                    dve.scalar_tensor_tensor(out=t1[:, :, :], in0=t0[:, :, :], scalar=0.5, in1=xcs[:, k % 4],
                                             op0=ALU.mult, op1=ALU.mult).then_inc(dve_sp, 1)

            def c_part(s, k, n):
                if n != 3:
                    return
                G = s * NC8 + k
                dve.wait_ge(pe_red, count(pe_red, (G + 1) * NU))
                dve.wait_ge(pe_out, count(pe_out, G))
                for t in range(2):
                    dve.scalar_tensor_tensor(out=yy[:, t, :], in0=xcs[:, k % 4, t, :], scalar=dhalf[:, t:t + 1],
                                             in1=py[0:C, t, :], op0=ALU.mult, op1=ALU.add).then_inc(dve_y, 1)
                dve.wait_ge(dve_zs, count(dve_zs, G + 1))
                dve.wait_ge(dve_y, count(dve_y, G * 3 + 2))
                dve.tensor_tensor(yy[:, :, :], yy[:, :, :], zs[:, :, :], ALU.mult).then_inc(dve_y, 1)

            run(nc.vector, MULT["dve"], 1, unit, step, lambda st: None, a_part, c_part)

        @block.gpsimd
        def _(pool):
            pool.wait_ge(zset, count(zset, 3))

            def step(st, i):
                name = st.plan[i][1][0]
                if name in ("SG2", "DG2"):
                    v = int(name == "DG2")
                    x = stage_sample(st, name)
                    pool.wait_ge(cb_free[(i) % 2], st.freed(i))
                    if v:
                        pool.wait_ge(act_gn, count(act_gn, x))
                    gn = gn1 if v else gnx
                    pool.tensor_tensor(gn[:, 0:1], ve[:, v:v + 1], mhalf[:, :], ALU.pow)\
                        .then_inc(pool_d if v else pool_s, 1)

            def unit(s, k, n):
                G = s * NC8 + k
                q, j = n // NJ, n % NJ
                if j == 0:
                    pool.wait_ge(act_c, count(act_c, G * NQ + q + 1))
                pool.wait_ge(dve_h, count(dve_h, G * NU + n + 1))
                pool.wait_ge(pe_red, count(pe_red, G * NU + n - 3))
                pool.tensor_tensor(hc[:, n % 4, :], bu[:, n // 2 % 4, n % 2, :], cs[:, q % 2, :], ALU.mult)\
                    .then_inc(pool_hc, 1)

            def a_part(s, k, n):
                G = s * NC8 + k
                if n == 18:
                    pool.wait_ge(dve_sp, count(dve_sp, G * 3 + 1))
                    pool.tensor_tensor(t2[:, :, :], t2[:, :, :], t1[:, :, :], ALU.subtract).then_inc(pool_sp, 1)
                if n == 19:
                    pool.wait_ge(pool_sp, count(pool_sp, G * 2 + 1))
                    pool.wait_ge(act_sp, count(act_sp, G * 3 + 3))
                    pool.tensor_tensor(t2[:, :, :], t0[:, :, :], t2[:, :, :], ALU.subtract).then_inc(pool_sp, 1)

            run(nc.gpsimd, MULT["pool"], 1, unit, step, lambda st: None, a_part, lambda s, k, n: None)


def resampling():
    k = np.arange(-31, 32)

    def up(n):
        j, w = np.arange(n)[:, None], np.arange(64)[None, :]
        a = np.exp(2j * np.pi * k * (j / n - w / 64)[..., None]).sum(-1).real
        return (a + 2 * np.cos(2 * np.pi * 32 * j / n) * (-1.0) ** w) / 64

    def down(n):
        i, j = np.arange(64)[:, None], np.arange(n)[None, :]
        a = np.exp(2j * np.pi * k * (i / 64 - j / n)[..., None]).sum(-1).real
        return (a + np.cos(2 * np.pi * 32 * j / n) * (-1.0) ** i) / n

    up_w = np.zeros((128, 2, GW), np.float32)
    up_h = np.zeros((128, 2 * GH), np.float32)
    for r in range(2):
        up_w[64 * r:64 * r + 64, r] = up(GW).T
        up_h[64 * r:64 * r + 64, GH * r:GH * r + GH] = up(GH).T
    dn_w = np.zeros((GW, 96), np.float32)
    dn_w[:, 0:64] = down(GW).T
    return up_w, up_h, down(GH).T.astype(np.float32), dn_w


def selectors():
    sel = np.zeros((96, 2 * NQ, 128), np.float32)
    for q in range(2 * NQ):
        for m in range(128):
            for part in range(3):
                sel[32 * part + 4 * q + m // 32, q, m] = 1
    rsel = np.tile(np.eye(32, dtype=np.float32), (4, 1))
    return sel.reshape(96, -1), rsel


def kernel(**inputs):
    import concourse.bacc as bacc
    from concourse.bass_utils import run_bass_kernel_spmd

    g = {k: np.asarray(v) for k, v in inputs.items()}
    up_w, up_h, dn_h, dn_w = resampling()
    sel, rsel = selectors()
    wx = g["L1_conv_W_x"]
    arrays = {
        "x": g["x"],
        "W1": g["L0_conv_W1"], "W1T": g["L0_conv_W1"].T, "b1": g["L0_conv_b1"].reshape(NF, 128).T,
        "W2T": g["L0_conv_W2"].T, "b2": g["L0_conv_b2"], "coef": g["L0_conv_coef"],
        "WinT": g["L1_conv_W_in"].T, "conv_w": g["L1_conv_conv_w"].reshape(2, 288), "conv_b": g["L1_conv_conv_b"],
        "WxT": np.concatenate([wx[RANK:], wx[:RANK]], 0).T, "WdtT": g["L1_conv_W_dt"].T,
        "b_dt": g["L1_conv_b_dt"], "D": g["L1_conv_D"].reshape(2, C).T, "WoT": g["L1_conv_W_out"].T,
        "A_lay": g["L1_conv_A_log"].reshape(NJ, 32, NQ, 4).transpose(3, 1, 2, 0).reshape(128, NQ, NJ),
        "up_w": up_w, "up_h": up_h, "dn_h": dn_h, "dn_w": dn_w, "sel": sel, "rsel": rsel,
        "ident": np.eye(128, dtype=np.float32),
        "gavg": np.kron(np.eye(C // GROUP), np.full((GROUP, GROUP), 1.0 / GROUP)).astype(np.float32),
    }
    arrays = {f"in_{k}": np.ascontiguousarray(v) for k, v in arrays.items()}
    nc = bacc.Bacc("TRN2", target_bir_lowering=False, num_devices=1)
    aps = {k[3:]: nc.dram_tensor(k, a.shape, mybir.dt.from_np(a.dtype), kind="ExternalInput").ap()
           for k, a in arrays.items()}
    aps["out"] = nc.dram_tensor("out", (NS, HH, WW, C), F32, kind="ExternalOutput").ap()
    build(nc, aps)
    r = run_bass_kernel_spmd(nc, [arrays], core_ids=[0])
    return r.results[0]["out"]
```

```python
from contextlib import ExitStack

import numpy as np

import concourse.bass as bass
from concourse import mybir

F32 = mybir.dt.float32
BF16 = mybir.dt.bfloat16
ALU = mybir.AluOpType
ACT = mybir.ActivationFunctionType

NS, HH, WW, C = 16, 64, 64, 96
L = HH * WW
GROUP = 3
HID = 384
NF = HID // 128
GW, GH = 100, 98
NB = GW // 4
BC = 4 * GH
DI, DSTATE, RANK = 192, 16, 6
T = 512
NC8 = L // T
NJ, NQ = DI // 32, DSTATE // 4
NU = NJ * NQ
NHC, NAV = 4, 6
XB_H = 8
LEAD = 2

AT = {
    "pe": dict(x=2, z=6, dbc=12, dt=16, out=8, spread=3, spreadb=0),
    "act": dict(xn=0, x=9, z=11, dbc=15, mid=18, sp=19, out=11, c=1, conv=5, b=3),
    "dve": dict(x=11, z=13, rest=15, lo=16, e1=18, delta=23, y=3, conv=5),
    "pool": dict(sp1=18, sp2=18),
    "sp": dict(x1=14, delta=22, spread=1, out=12),
}
LAG = {"pe": 0, "act": 3, "dve": 2, "pool": 1, "sp": 1}


def s_steps():
    out = []
    for b in range(HH // XB_H):
        out += [("ST", b), ("SA", b), ("SB", b)]
    return out + [("SG1", 0), ("SG2", 0)]


def w_steps():
    out = [("WG", 0)]
    for b in range(NB + 3):
        if b < NB:
            out.append(("W_up", b))
        if 1 <= b <= NB:
            out += [("W_f", b - 1, f) for f in range(NF)]
        if 2 <= b <= NB + 1:
            out.append(("W_2", b - 2))
        if b >= 3:
            out.append(("W_dn", b - 3))
    return out + [("WPAD", 0)]


def d_steps():
    out = [("DG", 0)]
    for k in range(NC8):
        out += [("D_lo", k), ("D_hi", k)]
    return out + [("DG1", 0), ("DG2", 0), ("DPAD", 0)]


def merged(d, w, s):
    rows = []
    for use, steps, begin, end in ((d, d_steps(), 0.0, 0.62), (w, w_steps(), 0.0, 1.0), (s, s_steps(), 0.0, 1.0)):
        if use:
            n = len(steps)
            rows += [(begin + (i / n) * (end - begin), st) for i, st in enumerate(steps)]
    rows.sort(key=lambda r: r[0])
    if d and w and s:
        return [(i * NC8 * NU // len(rows), st) for i, (_, st) in enumerate(rows)]
    return [(int(p * NC8 * NU), st) for p, st in rows]


def build(nc, A):
    ctx = ExitStack()
    with ctx:
        def sb(name, shape, dt=F32):
            return ctx.enter_context(nc.sbuf_tensor(name, shape, dt))

        def ps(name, shape):
            return ctx.enter_context(nc.psum_tensor(name, shape, F32))

        def sem(name):
            return ctx.enter_context(nc.semaphore(name))

        t1_d = nc.dram_tensor("t1_scratch", [NS, GW, HH * C], F32, kind="Internal").ap()
        v2_d = nc.dram_tensor("v2_scratch", [NS, HH, GW, C], F32, kind="Internal").ap()
        xt_d = nc.dram_tensor("xt_scratch", [NS, C, L], F32, kind="Internal").ap()
        x1_d = nc.dram_tensor("x1_scratch", [NS, C, L], F32, kind="Internal").ap()
        dl_d = nc.dram_tensor("delta_scratch", [2, DI, T], F32, kind="Internal").ap()
        du_d = nc.dram_tensor("deltax_scratch", [2, DI, T], F32, kind="Internal").ap()

        up_w = sb("up_w", [128, 2, GW])
        up_h = sb("up_h", [128, 2 * GH])
        dn_h = sb("dn_h", [GH, HH])
        dn_w = sb("dn_w", [GW, 96])
        ident = sb("ident", [128, 128])
        gavg = sb("gavg", [C, C])
        w1t = sb("w1t", [C, HID])
        w1a = sb("w1a", [C, HID])
        w2c = sb("w2c", [128, NF, C])
        b1t = sb("b1t", [128, NF])
        coef = sb("coef", [128, NF, 3])
        fcst = sb("fcst", [128, NF])
        b2t = sb("b2t", [C, 1])
        wlin = sb("wlin", [C, C])
        wtot = sb("wtot", [C, C])
        cbase = sb("cbase", [C, 1])
        win = sb("win", [C, 2 * DI])
        taps = sb("taps", [C, 2, 3])
        tapb = sb("tapb", [C, 2])
        wx = sb("wx", [C, 2, C])
        wdt = sb("wdt", [C + 1, DI])
        wo = sb("wo", [C, 2, C])
        nega = sb("nega", [128, NQ, NJ])
        dhalf = sb("dhalf", [C, 2])
        selb = sb("selb", [C, 2 * NQ, 128], BF16)
        rsel = sb("rsel", [128, 32])

        xb = sb("xb", [128, 2, 4, C])
        t1s = sb("t1s", [GW, XB_H, C])
        t1r = sb("t1r", [128, 2, 5, C])
        xu = sb("xu", [C, 2, BC])
        g2 = sb("g2", [128, 2, NF, BC])
        vr = sb("vr", [GH, 2, 4 * C])
        v2s = sb("v2s", [HH, 2, 4 * C])
        rr = sb("rr", [GW, 2, 4, C])
        xs = sb("xs", [C, T])
        xt = sb("xt", [C, 2, T])
        x1s = sb("x1s", [C, 2, T])
        bst = sb("bst", [C, 2, 8, 6])
        mv = sb("mv", [C, 2, 2])
        mg = sb("mg", [C, 2])
        dm = sb("dm", [C, 2])
        vv = sb("vv", [C, 2])
        ve = sb("ve", [C, 2])
        mhalf = sb("mhalf", [C, 1])
        zero2 = sb("zero2", [C, 2, 2])
        gnx = sb("gnx", [C, 2])
        gnd = sb("gnd", [C, 2])
        gn1 = sb("gn1", [C, 2])
        gna = sb("gna", [C, 2])
        b1a = sb("b1a", [128, NF])
        cst = sb("cst", [C, 1])

        x1c = sb("x1c", [C, 4, T])
        xn = sb("xn", [C, 4, T])
        xh = sb("xh", [C, 2, T + 2])
        xcs = sb("xcs", [C, 4, 2, T])
        zs = sb("zs", [C, 2, T])
        t0 = sb("t0", [C, 2, T])
        t1 = sb("t1", [C, 2, T])
        t2 = sb("t2", [C, 2, T])
        dbc = sb("dbc", [C + 1, T])
        bc3 = sb("bc3", [C, 4, T], BF16)
        rep_d = sb("rep_d", [128, 2, NJ, T])
        rep_u = sb("rep_u", [128, 2, NJ, T])
        bs = sb("bs", [128, 2, T])
        cs = sb("cs", [128, 2, T])
        av = sb("av", [128, NAV, T])
        bu = sb("bu", [128, 4, 2, T])
        hc = sb("hc", [128, NHC, T])
        w2t = hc[:, 0, 0:NF * C].rearrange("p (f c) -> p f c", f=NF)
        state = sb("state", [128, NQ, NJ])
        zero_state = sb("zero_state", [128, 1])
        os_ = sb("os_", [128, 4, C])

        cb = ps("cb", [128, 2, 512])
        px = ps("px", [128, 2, 512])
        pb = ps("pb", [128, 512])
        pm = ps("pm", [128, 512])
        py = ps("py", [128, 2, 512])

        ld_w = sem("ld_w")
        sp_passed = sem("sp_passed")
        zset = sem("zset")
        setup_v = sem("setup_v")
        setup_a = sem("setup_a")
        pe_conv = sem("pe_conv")
        cb_free = [sem("cb_free0"), sem("cb_free1")]
        xb_ld = [sem("xb_ld0"), sem("xb_ld1")]
        t1_st = sem("t1_st")
        t1_ld = [sem("t1_ld0"), sem("t1_ld1")]
        v2_st = [sem("v2_st0"), sem("v2_st1")]
        rr_ld = [sem("rr_ld0"), sem("rr_ld1")]
        xs_bn = sem("xs_bn")
        xt_st = sem("xt_st")
        xt_ld = [sem("xt_ld0"), sem("xt_ld1")]
        x1_st = [sem("x1_st0"), sem("x1_st1")]
        dve_s = sem("dve_s")
        dve_w = sem("dve_w")
        dve_d = sem("dve_d")
        x1_bn = sem("x1_bn")
        pool_s = sem("pool_s")
        pool_d = sem("pool_d")
        act_gn = sem("act_gn")
        x1c_ld = [sem(f"x1c_ld{i}") for i in range(4)]
        act_conv = sem("act_conv")
        dve_tap = sem("dve_tap")
        dve_conv = sem("dve_conv")
        act_xn = sem("act_xn")
        pe_x = sem("pe_x")
        act_tx = sem("act_tx")
        dve_xcs = sem("dve_xcs")
        pe_z = sem("pe_z")
        act_tz = sem("act_tz")
        dve_zs = sem("dve_zs")
        pe_dbc = sem("pe_dbc")
        act_dbc = sem("act_dbc")
        dve_bc = sem("dve_bc")
        pe_dt = sem("pe_dt")
        act_sp = sem("act_sp")
        dve_sp = sem("dve_sp")
        pool_sp = sem("pool_sp")
        dl_st = sem("dl_st")
        du_st = sem("du_st")
        rd_ld = [sem("rd_ld0"), sem("rd_ld1")]
        ru_ld = [sem("ru_ld0"), sem("ru_ld1")]
        pe_b = sem("pe_b")
        pe_c = sem("pe_c")
        act_b = sem("act_b")
        act_c = sem("act_c")
        act_a = sem("act_a")
        dve_bu = sem("dve_bu")
        dve_h = sem("dve_h")
        pool_stt = sem("pool_stt")
        pool_hc = sem("pool_hc")
        pe_red = sem("pe_red")
        dve_y = sem("dve_y")
        pe_out = sem("pe_out")
        act_out = sem("act_out")
        out_st = sem("out_st")

        xtok = A["x"].rearrange("s h w c -> s (h w) c")
        otok = A["out"].rearrange("s h w c -> s (h w) c")

        def tok(ap, s, t0_, n):
            v = ap[bass.ds(val(s), 1), t0_:t0_ + n, :].rearrange("o t c -> (o t) c")
            return v.rearrange("(i p) c -> p i c", p=128)

        loads = [
            (up_w[:, :, :], A["up_w"]), (up_h[:, :], A["up_h"]), (dn_h[:, :], A["dn_h"]),
            (dn_w[:, :], A["dn_w"]), (ident[:, :], A["ident"]), (gavg[:, :], A["gavg"]),
            (w1t[:, :], A["W1T"]), (w2t[:, :, :], A["W2T"].rearrange("(f p) c -> p f c", p=128)),
            (g2[:, 0, :, 0:C], A["W1"].rearrange("(f p) c -> p f c", p=128)),
            (b1t[:, :], A["b1"]),
            (coef[:, :, :], A["coef"].rearrange("(f p) k -> p f k", p=128)),
            (b2t[:, :], A["b2"].rearrange("(c o) -> c o", o=1)),
            (win[:, :], A["WinT"]),
            (wo[:, :, :], A["WoT"].rearrange("(t p) e -> p t e", p=C)),
            (nega[:, :, :], A["A_lay"]),
            (dhalf[:, :], A["D"]),
            (av[0:C, 0:2, :], A["sel"].rearrange("p (a b) -> p a b", a=2)),
            (rsel[:, :], A["rsel"]),
            (taps[:, :, :], A["conv_w"]), (tapb[:, :], A["conv_b"]),
            (wx[:, :, 0:RANK + 2 * DSTATE], A["WxT"].rearrange("(t p) e -> p t e", p=C)),
            (wdt[C:C + 1, :], A["b_dt"].rearrange("(o d) -> o d", o=1)),
            (wdt[32:32 + RANK, :], A["WdtT"]),
        ]
        N_FREE = len(loads) - 3

        PRE = [merged(0, 0, 1), merged(0, 1, 1), merged(1, 1, 1)]
        FULL = merged(1, 1, 1)
        TAIL = [merged(1, 1, 0), merged(1, 0, 0), []]
        SETUP_STEPS = 2
        N_SETUP = 12
        starts = [SETUP_STEPS]
        for m in PRE:
            starts.append(starts[-1] + len(m))
        LOOPS = NS - len(TAIL)
        UF = len(FULL)
        base_full = starts[len(PRE)]
        base_tail = base_full + LOOPS * UF
        assert UF % 2 == 0 and all(len(m) % 2 == 0 for m in PRE + TAIL), [len(m) for m in PRE]

        class Count:

            def __init__(self, multiples, m=1, c=0):
                self.multiples, self.m, self.c = multiples, m, c

            def __add__(self, c):
                if isinstance(c, Count):
                    return Count(self.multiples, self.m + c.m, self.c + c.c)
                return Count(self.multiples, self.m, self.c + c)

            __radd__ = __add__

            def __sub__(self, c):
                return self + -c

            def __mul__(self, m):
                return Count(self.multiples, self.m * m, self.c * m)

            __rmul__ = __mul__

        def val(v):
            return v.multiples[v.m] + v.c if isinstance(v, Count) else v

        class Steps:

            def __init__(self, plan, base, s):
                self.plan, self.base, self.s = plan, base, s
                self.at = {st: i for i, (_, st) in enumerate(plan)}

            def done(self, i):
                return val(self.base + i + 1)

            def freed(self, i):
                return val(self.half(i))

            def freed_all(self, steps):
                last = [max([i for i in steps if i % 2 == p], default=None) for p in range(2)]
                return [(cb_free[p], self.freed(i)) for p, i in enumerate(last) if i is not None]

            def half(self, i):
                if isinstance(self.base, int):
                    return (self.base + i) // 2 + 1
                return self.s * (UF // 2) + (base_full // 2 + i // 2 + 1)


        def run(eng, multiples, lag, unit_fn, step_fn, begin_fn, a_fn, c_fn):
            for it, plan in enumerate(PRE):
                st = Steps(plan, starts[it], it - len(PRE))
                begin_fn(st)
                for i in range(len(plan)):
                    step_fn(st, i)
                    if it == len(PRE) - 1:
                        d_end = st.at[("DPAD", 0)]
                        share = [max(x - d_end, 0) * LEAD * NU // (len(plan) - 1 - d_end) for x in (i - 1, i)]
                        for u in range(*share):
                            a_fn(0, u // NU, u % NU)

            def iteration(s, plan, base, first, last):
                st = Steps(plan, base, s)
                begin_fn(st)
                i = 0
                for k in range(NC8):
                    for n in range(NU):
                        unit_fn(s, k, n)
                        if k > 0:
                            c_fn(s, k - 1, n)
                        elif not first:
                            c_fn(s - 1, NC8 - 1, n)
                        ka = k + LEAD
                        if ka < NC8:
                            a_fn(s, ka, n)
                        elif not last:
                            a_fn(s + 1, ka - NC8, n)
                        while i < len(plan) and plan[i][0] + lag <= k * NU + n:
                            step_fn(st, i)
                            i += 1
                for i in range(i, len(plan)):
                    step_fn(st, i)

            iteration(0, FULL, base_full, True, False)
            with eng.Fori(1, LOOPS) as sample:
                s = Count({m: eng.snap(sample * m) if m > 1 else sample for m in multiples})
                iteration(s, FULL, s * UF + base_full, False, False)
            base = base_tail
            for t, plan in enumerate(TAIL):
                iteration(LOOPS + t, plan, base, False, t == len(TAIL) - 1)
                base += len(plan)
            for n in range(NU):
                c_fn(NS - 1, NC8 - 1, n)

        def count(sm, v):
            if isinstance(v, int):
                v = max(v, 0)
            return val(v)

        def stage_sample(st, name):
            return st.s + {"S": 3, "W": 2, "D": 1}[name[0]]

        MULT = {
            "sp": [1, 8, 24, 64, 96, UF // 2, 128, 192, UF, 208, 256],
            "pe": [2, 4, 5, 8, 16, 24, 32, 64, 80, 96, UF // 2, 128, 192, UF],
            "act": [1, 2, 96, 4, 5, 8, 16, 24, 32, 64, UF // 2, 128, 192, UF, 208, 256],
            "dve": [1, 2, 4, 5, 8, 16, 24, 32, 96, UF // 2, 128, 192, UF, 256],
            "pool": [1, 16, 24, 32, UF // 2, 192, UF],
        }

        block = ctx.enter_context(nc.Block())

        @block.sync
        def _(sp):
            for dst, src in loads[:N_FREE]:
                sp.dma_start(dst, src).then_inc(ld_w, 16)
            sp.wait_ge(zset, count(zset, 3))
            sp.sem_inc(sp_passed, 1)
            for dst, src in loads[N_FREE:]:
                sp.dma_start(dst, src).then_inc(ld_w, 16)

            def load_xb(st, b):
                x = stage_sample(st, "S")
                sp.dma_start(xb[:, b % 2], tok(xtok, x, b * T, T)).then_inc(xb_ld[b % 2], 16)

            def load_t1(st, m):
                w = stage_sample(st, "W")
                src = t1_d[bass.ds(val(w), 1)].rearrange("o w f -> (o w f)").rearrange(
                    "(i p c) -> p i c", p=128, c=C)[:, 5 * m:5 * m + 5, :]
                sp.dma_start(t1r[:, m % 2], src).then_inc(t1_ld[m % 2], 16)

            def load_rr(st, m):
                d = stage_sample(st, "D")
                src = v2_d[bass.ds(val(d), 1), 4 * m:4 * m + 4].rearrange("o h w c -> (o h) w c").rearrange(
                    "h w c -> w h c")
                sp.dma_start(rr[:, m % 2], src).then_inc(rr_ld[m % 2], 16)

            def load_xt(st, k):
                d = stage_sample(st, "D")
                src = xt_d[bass.ds(val(d), 1), :, k * T:(k + 1) * T].rearrange("o c t -> (o c) t")
                sp.dma_start(xt[:, k % 2], src).then_inc(xt_ld[k % 2], 16)

            def begin(st):
                if not st.plan:
                    return
                sp.wait_ge(pe_conv, count(pe_conv, st.base))
                sp.sem_inc(sp_passed, 1)
                if ("ST", 0) in st.at:
                    load_xb(st, 0)
                    load_xb(st, 1)
                if ("WG", 0) in st.at:
                    w = stage_sample(st, "W")
                    sp.wait_ge(t1_st, count(t1_st, (w + 1) * 128))
                    sp.sem_inc(sp_passed, 1)
                    load_t1(st, 0)
                    load_t1(st, 1)
                if ("DG", 0) in st.at:
                    d = stage_sample(st, "D")
                    sp.wait_ge(v2_st[0], count(v2_st[0], (d + 1) * (16 * 13)))
                    sp.sem_inc(sp_passed, 1)
                    sp.wait_ge(v2_st[1], count(v2_st[1], (d + 1) * (16 * 12)))
                    sp.sem_inc(sp_passed, 1)
                    sp.wait_ge(xt_st, count(xt_st, (d + 1) * 128))
                    sp.sem_inc(sp_passed, 1)
                    for m in range(2):
                        load_rr(st, m)
                        load_xt(st, m)

            def step(st, i):
                name, b = st.plan[i][1][:2]
                if name == "SB":
                    x = stage_sample(st, "S")
                    for bank_free, n_free in st.freed_all([i, st.at[("SA", b)]]):
                        sp.wait_ge(bank_free, n_free)
                        sp.sem_inc(sp_passed, 1)
                    dst = t1_d[bass.ds(val(x), 1), :, b * XB_H * C:(b + 1) * XB_H * C].rearrange(
                        "o w f -> (o w) f")
                    sp.dma_start(dst, t1s[:, :, :].rearrange("p h c -> p (h c)"))\
                        .then_inc(t1_st, 16)
                    if b + 2 < HH // XB_H:
                        sp.wait_ge(pe_conv, st.done(i))
                        sp.sem_inc(sp_passed, 1)
                        load_xb(st, b + 2)
                if name == "W_up":
                    for m in range(10):
                        if (5 * m + 4) // 2 == b and m + 2 < 10:
                            sp.wait_ge(pe_conv, st.done(i))
                            sp.sem_inc(sp_passed, 1)
                            load_t1(st, m + 2)
                if name == "W_dn":
                    w = stage_sample(st, "W")
                    sp.wait_ge(cb_free[(i) % 2], st.freed(i))
                    sp.sem_inc(sp_passed, 1)
                    dst = v2_d[bass.ds(val(w), 1), :, 4 * b:4 * b + 4, :].rearrange("o h w c -> (o h) (w c)")
                    sp.dma_start(dst, v2s[:, b % 2]).then_inc(v2_st[b % 2], 16)
                if name == "ST":
                    x = stage_sample(st, "S")
                    sp.wait_ge(cb_free[i % 2], st.freed(i))
                    sp.sem_inc(sp_passed, 1)
                    dst = xt_d[bass.ds(val(x), 1), :, b * T:(b + 1) * T].rearrange("o c t -> (o c) t")
                    sp.dma_start(dst, xs[:, :]).then_inc(xt_st, 16)
                if name in ("D_lo", "D_hi"):
                    m = 2 * b + (name == "D_hi")
                    if m + 2 < 2 * NC8:
                        sp.wait_ge(pe_conv, st.done(i))
                        sp.sem_inc(sp_passed, 1)
                        load_rr(st, m + 2)
                if name == "D_hi" and b + 2 < NC8:
                    load_xt(st, b + 2)
                if name == "D_hi":
                    d = stage_sample(st, "D")
                    for bank_free, n_free in st.freed_all([i, st.at[("D_lo", b)]]):
                        sp.wait_ge(bank_free, n_free)
                        sp.sem_inc(sp_passed, 1)
                    dst = x1_d[bass.ds(val(d), 1), :, b * T:(b + 1) * T].rearrange("o c t -> (o c) t")
                    sp.dma_start(dst, x1s[:, b % 2]).then_inc(x1_st[b % 2], 16)

            def load_x1c(s, k):
                for p in range(2):
                    sp.wait_ge(x1_st[p], count(x1_st[p], (s + 1) * 64))
                    sp.sem_inc(sp_passed, 1)
                sp.wait_ge(pe_out, count(pe_out, s * NC8 + k - 3))
                sp.sem_inc(sp_passed, 1)
                src = x1_d[bass.ds(val(s), 1), :, k * T:(k + 1) * T].rearrange("o c t -> (o c) t")
                sp.dma_start(x1c[:, k % 4], src).then_inc(x1c_ld[k % 4], 16)

            def a_part(s, k, n):
                G = s * NC8 + k
                if n == 0 and isinstance(G, int) and G == 0:
                    load_x1c(s, k)
                if n == AT["sp"]["x1"] and not (isinstance(G, int) and G + 1 == NS * NC8):
                    load_x1c(s + (k + 1) // NC8, (k + 1) % NC8)
                if n == AT["sp"]["delta"]:
                    sp.wait_ge(dve_sp, count(dve_sp, G * 3 + 2))
                    sp.sem_inc(sp_passed, 1)
                    for ld in (rd_ld, ru_ld):
                        sp.wait_ge(ld[k % 2], count(ld[k % 2], s * (4 * 64) + (k // 2) * 64))
                        sp.sem_inc(sp_passed, 1)
                    sp.dma_start(dl_d[k % 2].rearrange("(t p) f -> p t f", p=C), t0[:, :, :])\
                        .then_inc(dl_st, 16)
                    sp.wait_ge(dve_sp, count(dve_sp, G * 3 + 3))
                    sp.sem_inc(sp_passed, 1)
                    sp.dma_start(du_d[k % 2].rearrange("(t p) f -> p t f", p=C), t1[:, :, :])\
                        .then_inc(du_st, 16)

            def spread(s, k):
                G = s * NC8 + k
                sp.wait_ge(dl_st, count(dl_st, (G + 1) * 16))
                sp.sem_inc(sp_passed, 1)
                sp.wait_ge(act_a, count(act_a, (G - 1) * NU))
                sp.sem_inc(sp_passed, 1)
                for r in range(4):
                    sp.dma_start(rep_d[32 * r:32 * r + 32, k % 2],
                                 dl_d[k % 2].rearrange("(j p) f -> p j f", p=32))\
                        .then_inc(rd_ld[k % 2], 16)
                sp.wait_ge(du_st, count(du_st, (G + 1) * 16))
                sp.sem_inc(sp_passed, 1)
                sp.wait_ge(dve_bu, count(dve_bu, (G - 1) * (NU // 2)))
                sp.sem_inc(sp_passed, 1)
                for r in range(4):
                    sp.dma_start(rep_u[32 * r:32 * r + 32, k % 2],
                                 du_d[k % 2].rearrange("(j p) f -> p j f", p=32))\
                        .then_inc(ru_ld[k % 2], 16)

            def a_with_spread(s, k, n):
                a_part(s, k, n)
                if n == NU - 1 and isinstance(s, int) and s * NC8 + k < LEAD:
                    spread(s, k)

            def c_part(s, k, n):
                G = s * NC8 + k
                if n == AT["sp"]["spread"] and not (isinstance(G, int) and G + LEAD >= NS * NC8):
                    spread(s + (k + LEAD) // NC8, (k + LEAD) % NC8)
                if n != AT["sp"]["out"]:
                    return
                sp.wait_ge(act_out, count(act_out, G + 1))
                sp.sem_inc(sp_passed, 1)
                sp.dma_start(tok(otok, s, k * T, T), os_[:, :, :]).then_inc(out_st, 16)

            run(nc.sync, MULT["sp"], LAG["sp"], lambda s, k, n: None, step, begin, a_with_spread, c_part)
            sp.wait_ge(out_st, count(out_st, NS * NC8 * 16))
            sp.sem_inc(sp_passed, 1)
            sp.wait_ge(xt_st, count(xt_st, NS * 128))
            sp.sem_inc(sp_passed, 1)
            for p in range(2):
                sp.wait_ge(rd_ld[p], count(rd_ld[p], NS * NC8 // 2 * 64))
                sp.sem_inc(sp_passed, 1)
                sp.wait_ge(ru_ld[p], count(ru_ld[p], NS * NC8 // 2 * 64))
                sp.sem_inc(sp_passed, 1)

        @block.tensor
        def _(pe):
            pe.wait_ge(ld_w, count(ld_w, 16 * len(loads)))
            pe.wait_ge(setup_v, count(setup_v, 5))
            for f in range(NF):
                mm = pe.matmul(cb[0:C, 0, 0:C], g2[:, 0, f, 0:C], g2[:, 1, f, 0:C], start=(f == 0), stop=(f == NF - 1))
            mm.then_inc(pe_conv, 1)
            for f in range(NF):
                mm = pe.matmul(cb[0:C, 1, 0:1], w2t[:, f, :], fcst[:, f:f + 1], start=(f == 0), stop=(f == NF - 1))
            mm.then_inc(pe_conv, 1)
            pe.wait_ge(setup_v, count(setup_v, N_SETUP))
            pe.wait_ge(setup_a, count(setup_a, 3))

            def step(st, i):
                name, b = st.plan[i][1][:2]
                bank = cb[:, i % 2]
                x = stage_sample(st, name)
                at = st.at
                made = {"W_f": [("W_up", b), ("WG", 0)], "W_2": [("W_f", b, f) for f in range(NF)],
                        "W_dn": [("W_2", b)]}.get(name, [])
                for bank_free, n_free in st.freed_all([i - 2] + [at[m] for m in made]):
                    pe.wait_ge(bank_free, n_free)
                if name == "ST":
                    pe.wait_ge(xb_ld[b % 2], count(xb_ld[b % 2], x * 64 + (b // 2 + 1) * 16))
                    for j in range(4):
                        mm = pe.transpose(bank[0:C, 128 * j:128 * j + 128], xb[:, b % 2, j, :], ident[:, :])
                elif name in ("SA", "SB"):
                    mm = pe.matmul(bank[0:GW, 0:4 * C], up_w[:, int(name == "SB"), :],
                                   xb[:, b % 2].rearrange("p i c -> p (i c)"), start=True, stop=True)
                elif name in ("SG1", "DG1"):
                    v = int(name == "DG1")
                    pe.wait_ge(dve_d if v else dve_s, count(dve_d if v else dve_s, x * (5 if v else 4) + 1 + v))
                    mm = pe.matmul(bank[0:C, 0:1], gavg[:, :], mv[:, v, 0:1], start=True, stop=True)
                elif name in ("SG2", "DG2"):
                    v = int(name == "DG2")
                    pe.wait_ge(dve_d if v else dve_s, count(dve_d if v else dve_s, x * (5 if v else 4) + 3 + v))
                    mm = pe.matmul(bank[0:C, 0:1], gavg[:, :], vv[:, v:v + 1], start=True, stop=True)
                elif name == "WG":
                    pe.wait_ge(dve_s, count(dve_s, x * 4 + 4))
                    for f in range(NF):
                        mm = pe.matmul(bank[:, f:f + 1], w1t[:, 128 * f:128 * f + 128], gnx[:, 1:2],
                                       start=True, stop=True)
                elif name == "W_up":
                    for e in range(2):
                        i2 = 2 * b + e
                        m = i2 // 5
                        if i2 % 5 == 0 or e == 0:
                            pe.wait_ge(t1_ld[m % 2], count(t1_ld[m % 2], x * 80 + (m // 2 + 1) * 16))
                        mm = pe.matmul(bank[0:C, e * 2 * GH:(e + 1) * 2 * GH], t1r[:, m % 2, i2 % 5, :],
                                       up_h[:, :], start=True, stop=True)
                elif name == "W_f":
                    f = st.plan[i][1][2]
                    if f == 0:
                        pe.wait_ge(dve_w, count(dve_w, x * 2 + 2))
                    mm = pe.matmul(bank[:, 0:BC], w1a[:, 128 * f:128 * f + 128], xu[:, b % 2, :],
                                   start=True, stop=True)
                elif name == "W_2":
                    for j in range(4):
                        for f in range(NF):
                            mm = pe.matmul(bank[0:GH, C * j:C * j + C], g2[:, b % 2, f, GH * j:GH * j + GH],
                                           w2c[:, f, :], start=(f == 0), stop=(f == NF - 1))
                elif name == "W_dn":
                    mm = pe.matmul(bank[0:HH, 0:4 * C], dn_h[:, :], vr[:, b % 2, :], start=True, stop=True)
                elif name == "DG":
                    pe.wait_ge(dve_d, count(dve_d, x * 5 + 1))
                    mm = pe.matmul(bank[0:C, 0:1], wlin[:, :], gnd[:, 1:2], start=True, stop=True)
                elif name in ("D_lo", "D_hi"):
                    hf = int(name == "D_hi")
                    m = 2 * b + hf
                    if hf == 0:
                        pe.wait_ge(xt_ld[b % 2], count(xt_ld[b % 2], x * 64 + (b // 2 + 1) * 16))
                    pe.wait_ge(rr_ld[m % 2], count(rr_ld[m % 2], x * 128 + (m // 2 + 1) * 16))
                    o = bank[0:C, 0:4 * 96].rearrange("c (h w) -> c h w", h=4)
                    pe.matmul(o[:, :, 0:WW], wtot[:, :],
                              xt[:, b % 2, hf * 256:hf * 256 + 256].rearrange("c (h w) -> c h w", h=4),
                              start=True, stop=False, skip_group_check=True)
                    for j in range(4):
                        mm = pe.matmul(o[:, j, :], rr[:, m % 2, j, :], dn_w[:, :], start=False, stop=(j == 3),
                                       skip_group_check=True)
                elif name in ("DPAD", "WPAD"):
                    mm = pe.transpose(bank[0:C, 0:C], ident[0:C, 0:C], ident[0:C, 0:C])
                mm.then_inc(pe_conv, 1)

            def unit(s, k, n):
                G = s * NC8 + k
                q, j = n // NJ, n % NJ
                if isinstance(G, int) and G == 0 and n == 0:
                    spread_b(G, k, 0)
                    spread_c(G, k, 0)
                for place, spread in (("spreadb", spread_b), ("spread", spread_c)):
                    if j == AT["pe"][place]:
                        if q + 1 < NQ:
                            spread(G, k, q + 1)
                        elif not (isinstance(G, int) and G + 1 == NS * NC8):
                            spread(G + 1, (k + 1) % NC8, 0)
                for r in range(summed(n - 1), summed(n)):
                    reduce(s, k, r)
                if n == AT["pe"]["z"]:
                    zproj(s, k)

            def summed(n):
                return max(0, min(n - 2, 2 * (n - 3) + 1))

            def spread_b(G, k, q):
                if q == 0:
                    pe.wait_ge(dve_bc, count(dve_bc, G * 2 + 2))
                    pe.wait_ge(act_dbc, count(act_dbc, after_dbc(G + 1)))
                pe.wait_ge(act_b, count(act_b, G * NQ + q))
                pe.matmul(pb[:, :], selb[:, q, :], bc3[:, k % 4, :], start=True, stop=True).then_inc(pe_b, 1)

            def spread_c(G, k, q):
                if q == 0:
                    pe.wait_ge(dve_bc, count(dve_bc, G * 2 + 2))
                    pe.wait_ge(act_dbc, count(act_dbc, after_dbc(G + 1)))
                pe.wait_ge(act_c, count(act_c, G * NQ + q))
                if q == 2:
                    pe.wait_ge(act_out, count(act_out, G))
                if q == 3:
                    pe.wait_ge(act_dbc, count(act_dbc, after_dbc(G + 2)))
                pe.matmul(pm[:, :], selb[:, NQ + q, :], bc3[:, k % 4, :], start=True, stop=True).then_inc(pe_c, 1)

            def after_dbc(G):
                return NS * NC8 * 3 if isinstance(G, int) and G >= NS * NC8 else G * 3 + 2

            def reduce(s, k, n):
                G = s * NC8 + k
                q, j = n // NJ, n % NJ
                if n in (0, 3):
                    pe.wait_ge(dve_y, count(dve_y, (G - 1) * 3 + 1 + n // 3))
                pe.wait_ge(pool_hc, count(pool_hc, G * NU + n + 1))
                pe.matmul(py[32 * (j % 3):32 * (j % 3) + 32, j // 3, :], rsel[:, :], hc[:, n % NHC, :],
                          start=(q == 0), stop=(q == NQ - 1)).then_inc(pe_red, 1)

            def zproj(s, k):
                G = s * NC8 + k
                tail = isinstance(G, int) and G + 3 > NS * NC8
                pe.wait_ge(act_conv, count(act_conv, NS * NC8 * 4 if tail else (G + 3) * 4))
                pe.wait_ge(dve_sp, count(dve_sp, NS * NC8 * 3 if tail else (G + 2) * 3))
                for t in range(2):
                    mm = pe.matmul(px[0:C, t, :], win[:, DI + C * t:DI + C * t + C], xn[:, k % 4, :],
                                   start=True, stop=True)
                mm.then_inc(pe_z, 1)

            def a_part(s, k, n):
                G = s * NC8 + k
                if n == AT["pe"]["x"]:
                    pe.wait_ge(act_xn, count(act_xn, G + 1))
                    pe.wait_ge(dve_sp, count(dve_sp, G * 3))
                    pe.wait_ge(dve_zs, count(dve_zs, G - 2))
                    for t in range(2):
                        mm = pe.matmul(px[0:C, t, :], win[:, C * t:C * t + C], xn[:, k % 4, :], start=True, stop=True)
                    mm.then_inc(pe_x, 1)
                if n == AT["pe"]["dbc"]:
                    pe.wait_ge(dve_xcs, count(dve_xcs, G + 1))
                    pe.wait_ge(act_dbc, count(act_dbc, G * 3))
                    pe.wait_ge(act_c, count(act_c, (G - 2) * NQ + 3))
                    for t in range(2):
                        mm = pe.matmul(pm[0:C, :], wx[:, t, :], xcs[:, k % 4, t, :], start=(t == 0), stop=(t == 1))
                    mm.then_inc(pe_dbc, 1)
                if n == AT["pe"]["dt"]:
                    pe.wait_ge(act_dbc, count(act_dbc, G * 3 + 1))
                    pe.wait_ge(dve_zs, count(dve_zs, G - 1))
                    for t in range(2):
                        mm = pe.matmul(px[0:C, t, :], wdt[:, C * t:C * t + C], dbc[:, :], start=True, stop=True)
                    mm.then_inc(pe_dt, 1)

            def c_part(s, k, n):
                G = s * NC8 + k
                if n == 0:
                    for r in range(summed(NU - 1), NU):
                        reduce(s, k, r)
                if n != AT["pe"]["out"]:
                    return
                pe.wait_ge(dve_y, count(dve_y, G * 3 + 3))
                pe.wait_ge(act_c, count(act_c, NS * NC8 * NQ if isinstance(G, int) and G + 1 == NS * NC8
                                        else (G + 1) * NQ + 2))
                yy = xcs[:, k % 4]
                for b in range(4):
                    tb = slice(128 * b, 128 * b + 128)
                    o = pm[:, C * b:C * b + C]
                    for t in range(2):
                        pe.matmul(o, yy[:, t, tb], wo[:, t, :], start=(t == 0), stop=False)
                    mm = pe.matmul(o, x1c[:, k % 4, tb], ident[0:C, 0:C], start=False, stop=True)
                mm.then_inc(pe_out, 1)

            run(nc.tensor, MULT["pe"], LAG["pe"], unit, step, lambda st: None, a_part, c_part)

        @block.scalar
        def _(act):
            act.wait_ge(ld_w, count(ld_w, 16 * len(loads)))
            act.activation(selb[:, 0:NQ, :].rearrange("p q m -> p (q m)"), av[0:C, 0, :], ACT.Copy).then_inc(setup_a, 1)
            act.activation(selb[:, NQ:2 * NQ, :].rearrange("p q m -> p (q m)"), av[0:C, 1, :], ACT.Copy).then_inc(setup_a, 1)
            act.activation(nega[:, :, :], nega[:, :, :], ACT.Exp).then_inc(setup_a, 1)
            act.wait_ge(setup_v, count(setup_v, N_SETUP))

            def step(st, i):
                key = st.plan[i][1]
                name, b = key[:2]
                bank = cb[:, i % 2]
                x = stage_sample(st, name)
                out = None
                if name in ("SA", "SB"):
                    par = int(name == "SB")
                    if par == 0:
                        act.wait_ge(t1_st, count(t1_st, x * 128 + b * 16))
                    out = t1s[:, :, :].rearrange("p (i r) c -> p i r c", r=2)[:, :, par, :]
                    src = bank[0:GW, 0:4 * C].rearrange("p (i c) -> p i c", i=4)
                elif name == "W_up":
                    out, src = xu[:, b % 2, :], bank[0:C, 0:BC]
                elif name == "W_2":
                    out, src = vr[:, b % 2, :], bank[0:GH, 0:4 * C]
                elif name == "W_dn":
                    act.wait_ge(v2_st[b % 2], count(v2_st[b % 2], x * (16 * (13 - b % 2)) + (b // 2) * 16))
                    out, src = v2s[:, b % 2, :], bank[0:HH, 0:4 * C]
                elif name == "ST":
                    act.wait_ge(xt_st, count(xt_st, x * 128 + b * 16))
                    act.wait_ge(xs_bn, count(xs_bn, x * 8 + b))
                    out, src = xs[:, :], bank[0:C, :]
                if out is not None:
                    act.wait_ge(pe_conv, st.done(i))
                    act.activation(out, src, ACT.Copy).then_inc(cb_free[i % 2], 1)
                elif name == "W_f":
                    f = key[2]
                    act.wait_ge(pe_conv, st.done(i))
                    if b == 0 and f == 0:
                        act.wait_ge(cb_free[(st.at[("WG", 0)]) % 2], st.freed(st.at[("WG", 0)]))
                    act.activation(g2[:, b % 2, f, :], bank[:, 0:BC], ACT.Square, bias=b1a[:, f:f + 1])\
                        .then_inc(cb_free[i % 2], 1)
                elif name in ("D_lo", "D_hi"):
                    hf = int(name == "D_hi")
                    act.wait_ge(pe_conv, st.done(i))
                    if b == 0:
                        act.wait_ge(cb_free[(st.at[("DG", 0)]) % 2], st.freed(st.at[("DG", 0)]))
                    act.wait_ge(x1_st[b % 2], count(x1_st[b % 2], x * 64 + (b // 2) * 16))
                    act.wait_ge(x1_bn, count(x1_bn, x * 8 + b - 1))
                    act.activation(x1s[:, b % 2, 256 * hf:256 * hf + 256].rearrange("c (h w) -> c h w", h=4),
                                   bank[0:C, 0:384].rearrange("c (h w) -> c h w", h=4)[:, :, 0:WW],
                                   ACT.Identity, bias=cst[:, 0:1]).then_inc(cb_free[i % 2], 1)

            def unit(s, k, n):
                G = s * NC8 + k
                q, j = n // NJ, n % NJ
                if isinstance(G, int) and G == 0 and n == 0:
                    copy_b(G, 0)
                if n == 0:
                    act.wait_ge(rd_ld[k % 2], count(rd_ld[k % 2], s * (4 * 64) + (k // 2 + 1) * 64))
                act.wait_ge(dve_h, count(dve_h, G * NU + n + 1 - NAV))
                act.activation(av[:, n % NAV, :], rep_d[:, k % 2, j, :], ACT.Exp, scale=nega[:, q, j:j + 1])\
                    .then_inc(act_a, 1)
                if j == AT["act"]["b"]:
                    if q + 1 < NQ:
                        copy_b(G, q + 1)
                    elif not (isinstance(G, int) and G + 1 == NS * NC8):
                        copy_b(G + 1, 0)
                if j == AT["act"]["c"]:
                    act.wait_ge(pe_c, count(pe_c, G * NQ + q + 1))
                    act.wait_ge(pool_hc, count(pool_hc, G * NU + NJ * (q - 1)))
                    act.activation(cs[:, q % 2, :], pm[:, :], ACT.Copy).then_inc(act_c, 1)
                if n == AT["act"]["z"]:
                    act.wait_ge(pe_z, count(pe_z, G + 1))
                    act.wait_ge(dve_sp, count(dve_sp, NS * NC8 * 3 if isinstance(G, int) and G + 2 > NS * NC8 else (G + 2) * 3))
                    act.activation(t2[:, :, :], px[0:C, :, :], ACT.Tanh, scale=0.5).then_inc(act_tz, 1)

            def copy_b(G, q):
                act.wait_ge(pe_b, count(pe_b, G * NQ + q + 1))
                act.wait_ge(dve_bu, count(dve_bu, G * (NU // 2) + 3 * (q - 1)))
                act.activation(bs[:, q % 2, :], pb[:, :], ACT.Copy).then_inc(act_b, 1)

            def a_part(s, k, n):
                G = s * NC8 + k
                if n == AT["act"]["xn"]:
                    if k == 0:
                        act.wait_ge(dve_d, count(dve_d, s * 5 + 5))
                        act.wait_ge(pool_d, count(pool_d, s + 1))
                        act.activation(gna[:, :], gn1[:, :], ACT.Copy).then_inc(act_gn, 1)
                        act.wait_ge(act_gn, count(act_gn, s + 1))
                    act.wait_ge(x1c_ld[k % 4], count(x1c_ld[k % 4], s * 32 + (k // 4 + 1) * 16))
                    act.wait_ge(pe_z, count(pe_z, G - 3))
                    act.activation(xn[:, k % 4, :], x1c[:, k % 4, :], ACT.Identity,
                                   bias=gna[:, 1:2], scale=gna[:, 0:1]).then_inc(act_xn, 1)
                if n == AT["act"]["conv"]:
                    act.wait_ge(dve_conv, count(dve_conv, G * 2))
                    act.wait_ge(act_conv, count(act_conv, G * 4))
                    act.activation(xh[:, :, 0:2], zero2[:, :, :] if k == 0 else xh[:, :, T:T + 2], ACT.Copy)\
                        .then_inc(act_conv, 1)
                    act.wait_ge(pe_x, count(pe_x, G + 1))
                    act.wait_ge(act_conv, count(act_conv, G * 4 + 1))
                    act.activation(xh[:, :, 2:T + 2], px[0:C, :, :], ACT.Copy).then_inc(act_conv, 1)
                    act.wait_ge(pe_out, count(pe_out, G - 3))
                    for t in range(2):
                        act.activation(xcs[:, k % 4, t, :], px[0:C, t, :], ACT.Identity,
                                       bias=tapb[:, t:t + 1], scale=taps[:, t, 2:3]).then_inc(act_conv, 1)
                if n == AT["act"]["x"]:
                    act.wait_ge(dve_conv, count(dve_conv, G * 2 + 2))
                    act.wait_ge(du_st, count(du_st, G * 16))
                    act.activation(t1[:, :, :], xcs[:, k % 4], ACT.Tanh, scale=0.5).then_inc(act_tx, 1)
                if n == AT["act"]["dbc"]:
                    act.wait_ge(pe_dbc, count(pe_dbc, G + 1))
                    act.wait_ge(pe_dt, count(pe_dt, G))
                    act.wait_ge(dve_bc, count(dve_bc, G * 2))
                    act.activation(dbc[0:C, :], pm[0:C, :], ACT.Copy).then_inc(act_dbc, 1)
                    act.wait_ge(pe_c, count(pe_c, (G - 2) * NQ))
                    act.activation(bc3[0:32, k % 4, :], pm[0:32, :], ACT.Copy).then_inc(act_dbc, 1)
                if n == AT["act"]["mid"]:
                    act.wait_ge(dve_bc, count(dve_bc, G * 2 + 1))
                    act.activation(bc3[32:64, k % 4, :], t1[32:64, 0, :], ACT.Copy).then_inc(act_dbc, 1)
                if n == AT["act"]["sp"]:
                    act.wait_ge(pe_dt, count(pe_dt, G + 1))
                    act.wait_ge(dl_st, count(dl_st, G * 16))
                    act.wait_ge(du_st, count(du_st, G * 16))
                    act.activation(t0[:, :, :], px[0:C, :, :], ACT.Abs).then_inc(act_sp, 1)
                    act.wait_ge(act_sp, count(act_sp, G * 3 + 1))
                    act.wait_ge(dve_bc, count(dve_bc, G * 2 + 2))
                    act.activation(t1[:, :, :], t0[:, :, :], ACT.Exp, scale=-1.0).then_inc(act_sp, 1)
                    act.wait_ge(act_sp, count(act_sp, G * 3 + 2))
                    act.activation(t0[:, :, :], t1[:, :, :], ACT.Ln, bias=1.0).then_inc(act_sp, 1)

            def c_part(s, k, n):
                if n != AT["act"]["out"]:
                    return
                G = s * NC8 + k
                act.wait_ge(pe_out, count(pe_out, G + 1))
                act.wait_ge(out_st, count(out_st, G * 16))
                act.activation(os_[:, :, :].rearrange("p b c -> p (b c)"), pm[:, 0:4 * C], ACT.Copy).then_inc(act_out, 1)

            run(nc.scalar, MULT["act"], LAG["act"], unit, step, lambda st: None, a_part, c_part)

        @block.vector
        def _(dve):
            dve.memset(wx[:, :, :], 0.0).then_inc(zset, 1)
            dve.memset(wdt[:, :], 0.0).then_inc(zset, 1)
            dve.memset(dbc[C:C + 1, :], 1.0)
            dve.memset(mhalf[:, :], -0.5)
            dve.memset(zero_state[:, :], 0.0)
            dve.memset(zero2[:, :, :], 0.0).then_inc(zset, 1)
            dve.wait_ge(ld_w, count(ld_w, 16 * len(loads)))
            n_set = [0]

            def setup(ins):
                n_set[0] += 1
                ins.then_inc(setup_v, 1)
                dve.wait_ge(setup_v, count(setup_v, n_set[0]))

            for f in range(NF):
                setup(dve.tensor_scalar(g2[:, 1, f, 0:C], w2t[:, f, :], coef[:, f, 1:2], None, ALU.mult))
            setup(dve.tensor_tensor(fcst[:, :], b1t[:, :], coef[:, :, 1], ALU.mult))
            setup(dve.tensor_tensor(fcst[:, :], fcst[:, :], coef[:, :, 0], ALU.add))
            for f in range(NF):
                setup(dve.tensor_scalar(w2c[:, f, :], w2t[:, f, :], coef[:, f, 2:3], None, ALU.mult))
            setup(dve.tensor_scalar(wx[:, :, :], wx[:, :, :], 0.5, None, ALU.mult))
            setup(dve.tensor_scalar(wo[:, :, :], wo[:, :, :], 0.5, None, ALU.mult))
            setup(dve.tensor_scalar(dhalf[:, :], dhalf[:, :], 0.5, None, ALU.mult))
            dve.wait_ge(setup_a, count(setup_a, 3))
            setup(dve.tensor_scalar(nega[:, :, :], nega[:, :, :], -1.0, None, ALU.mult))
            dve.wait_ge(pe_conv, count(pe_conv, 2))
            dve.tensor_copy(wlin[:, :], cb[0:C, 0, 0:C]).then_inc(cb_free[0], 1)
            dve.tensor_tensor(cbase[:, :], cb[0:C, 1, 0:1], b2t[:, :], ALU.add).then_inc(cb_free[1], 1)
            assert n_set[0] == N_SETUP

            def step(st, i):
                name, b = st.plan[i][1][:2]
                bank = cb[:, i % 2]
                x = stage_sample(st, name)
                fr = cb_free[i % 2]
                if name == "ST":
                    dve.wait_ge(fr, st.freed(i))
                    dve.bn_stats(bst[:, 0, b, :], xs[:, :]).then_inc(xs_bn, 1)
                    if b == 7:
                        dve.wait_ge(xs_bn, count(xs_bn, x * 8 + 8))
                        dve.memset(dm[:, 0:1], 0.0)
                        dve.bn_aggr(mv[:, 0, :], bst[:, 0].rearrange("c a b -> c (a b)")).then_inc(dve_s, 1)
                elif name in ("SG1", "DG1"):
                    v = int(name == "DG1")
                    sm, c0 = (dve_d, x * 5 + 1) if v else (dve_s, x * 4)
                    dve.wait_ge(pe_conv, st.done(i))
                    dve.tensor_copy(mg[:, v:v + 1], bank[0:C, 0:1]).then_inc(fr, 1)
                    dve.wait_ge(cb_free[(i) % 2], st.freed(i))
                    dve.tensor_tensor(dm[:, v:v + 1], mv[:, v, 0:1], mg[:, v:v + 1], ALU.subtract).then_inc(sm, 1)
                    dve.wait_ge(sm, count(sm, c0 + 2))
                    dve.scalar_tensor_tensor(out=vv[:, v:v + 1], in0=dm[:, v:v + 1], scalar=dm[:, v:v + 1],
                                             in1=mv[:, v, 1:2], op0=ALU.mult, op1=ALU.add).then_inc(sm, 1)
                elif name in ("SG2", "DG2"):
                    v = int(name == "DG2")
                    sm, c0, pl, gn = (dve_d, x * 5 + 1, pool_d, gn1) if v else (dve_s, x * 4, pool_s, gnx)
                    dve.wait_ge(pe_conv, st.done(i))
                    dve.tensor_scalar(ve[:, v:v + 1], bank[0:C, 0:1], 1e-5, None, ALU.add).then_inc(fr, 1)
                    dve.wait_ge(pl, count(pl, x + 1))
                    dve.scalar_tensor_tensor(out=gn[:, 1:2], in0=mg[:, v:v + 1], scalar=-1.0, in1=gn[:, 0:1],
                                             op0=ALU.mult, op1=ALU.mult).then_inc(sm, 1)
                elif name == "WG":
                    dve.wait_ge(dve_s, count(dve_s, x * 4 + 4))
                    dve.wait_ge(cb_free[(i - 1) % 2], st.freed(i - 1))
                    dve.wait_ge(cb_free[(i - 2) % 2], st.freed(i - 2))
                    dve.tensor_scalar(w1a[:, :], w1t[:, :], gnx[:, 0:1], None, ALU.mult).then_inc(dve_w, 1)
                    dve.tensor_copy(gnd[:, :], gnx[:, :]).then_inc(dve_w, 1)
                    dve.wait_ge(pe_conv, st.done(i))
                    dve.tensor_tensor(b1a[:, :], bank[:, 0:NF], b1t[:, :], ALU.add).then_inc(fr, 1)
                elif name == "DG":
                    dve.wait_ge(cb_free[(i - 1) % 2], st.freed(i - 1))
                    dve.wait_ge(cb_free[(i - 2) % 2], st.freed(i - 2))
                    dve.wait_ge(pe_conv, st.done(i))
                    dve.tensor_tensor(cst[:, :], bank[0:C, 0:1], cbase[:, :], ALU.add).then_inc(fr, 1)
                elif name == "D_hi":
                    for bank_free, n_free in st.freed_all([i, st.at[("D_lo", b)]]):
                        dve.wait_ge(bank_free, n_free)
                    dve.bn_stats(bst[:, 1, b, :], x1s[:, b % 2, :]).then_inc(x1_bn, 1)
                    if b == 7:
                        dve.wait_ge(x1_bn, count(x1_bn, x * 8 + 8))
                        dve.memset(dm[:, 1:2], 0.0)
                        dve.bn_aggr(mv[:, 1, :], bst[:, 1].rearrange("c a b -> c (a b)")).then_inc(dve_d, 1)
                elif name in ("DPAD", "WPAD"):
                    dve.wait_ge(pe_conv, st.done(i))
                    dve.tensor_copy(dm[:, 1:2], bank[0:C, 0:1]).then_inc(fr, 1)

            def begin(st):
                if ("DG", 0) in st.at:
                    x = stage_sample(st, "D")
                    dve.wait_ge(dve_w, count(dve_w, x * 2 + 2))
                    dve.scalar_tensor_tensor(out=wtot[:, :], in0=wlin[:, :], scalar=gnd[:, 0:1], in1=ident[0:C, 0:C],
                                             op0=ALU.mult, op1=ALU.add).then_inc(dve_d, 1)

            def product(s, k, m):
                G = s * NC8 + k
                q, j = 2 * m // NJ, 2 * m % NJ
                if m == 0:
                    dve.wait_ge(ru_ld[k % 2], count(ru_ld[k % 2], s * (4 * 64) + (k // 2 + 1) * 64))
                if j == 0:
                    dve.wait_ge(act_b, count(act_b, G * NQ + q + 1))
                dve.wait_ge(pool_hc, count(pool_hc, G * NU + 2 * (m - 3)))
                dve.wait_ge(pool_stt, count(pool_stt, G * (NU // 2) + m - 3))
                dve.tensor_tensor(bu[:, m % 4], rep_u[:, k % 2, j:j + 2, :],
                                  bs[:, q % 2, None, :].broadcast_to([128, 2, T]), ALU.mult).then_inc(dve_bu, 1)

            def unit(s, k, n):
                G = s * NC8 + k
                q, j = n // NJ, n % NJ
                m = n // 2
                if n == 0:
                    product(s, k, 0)
                if n % 2 == 0 and m + 1 < NU // 2:
                    product(s, k, m + 1)
                dve.wait_ge(act_a, count(act_a, G * NU + n + 1))
                if n % 2 == 0:
                    dve.wait_ge(pool_stt, count(pool_stt, (G - 1) * (NU // 2) + m + 1))
                    dve.wait_ge(dve_bu, count(dve_bu, G * (NU // 2) + m + 1))
                h = bu[:, m % 4, n % 2, :]
                start = state[:, q, j:j + 1] if k > 0 else zero_state[:, 0:1]
                dve.tensor_tensor_scan(h, av[:, n % NAV, :], h, start, ALU.mult, ALU.add).then_inc(dve_h, 1)
                if n == AT["dve"]["z"]:
                    dve.wait_ge(act_tz, count(act_tz, G + 1))
                    dve.scalar_tensor_tensor(out=zs[:, :, :], in0=t2[:, :, :], scalar=1.0, in1=px[0:C, :, :],
                                             op0=ALU.add, op1=ALU.mult).then_inc(dve_zs, 1)

            def a_part(s, k, n):
                G = s * NC8 + k
                if n == AT["dve"]["conv"]:
                    dve.wait_ge(act_conv, count(act_conv, G * 4 + 4))
                    for tap in (1, 0):
                        if tap == 0:
                            dve.wait_ge(dve_tap, count(dve_tap, G * 2 + 2))
                        for t in range(2):
                            dve.scalar_tensor_tensor(out=xcs[:, k % 4, t, :], in0=xh[:, t, tap:tap + T],
                                                     scalar=taps[:, t, tap:tap + 1], in1=xcs[:, k % 4, t, :],
                                                     op0=ALU.mult, op1=ALU.add)\
                                .then_inc(dve_tap if tap == 1 else dve_conv, 1)
                if n == AT["dve"]["x"]:
                    dve.wait_ge(act_tx, count(act_tx, G + 1))
                    dve.scalar_tensor_tensor(out=xcs[:, k % 4], in0=t1[:, :, :], scalar=1.0, in1=xcs[:, k % 4],
                                             op0=ALU.add, op1=ALU.mult).then_inc(dve_xcs, 1)
                if n == AT["dve"]["rest"]:
                    dve.wait_ge(act_dbc, count(act_dbc, G * 3 + 2))
                    dve.wait_ge(du_st, count(du_st, G * 16))
                    dve.tensor_tensor(t1[32:64, 0, :], dbc[0:32, :], bc3[0:32, k % 4, :], ALU.subtract)\
                        .then_inc(dve_bc, 1)
                if n == AT["dve"]["lo"]:
                    dve.wait_ge(act_dbc, count(act_dbc, G * 3 + 3))
                    dve.tensor_tensor(bc3[64:96, k % 4, :], t1[32:64, 0, :], bc3[32:64, k % 4, :], ALU.subtract)\
                        .then_inc(dve_bc, 1)
                if n == AT["dve"]["e1"]:
                    dve.wait_ge(act_sp, count(act_sp, G * 3 + 2))
                    dve.wait_ge(dve_zs, count(dve_zs, G - 1))
                    dve.tensor_scalar(t2[:, :, :], t1[:, :, :], 1.0, 1.0, ALU.add, ALU.subtract).then_inc(dve_sp, 1)
                if n == AT["dve"]["delta"]:
                    dve.wait_ge(pool_sp, count(pool_sp, G * 2 + 2))
                    dve.scalar_tensor_tensor(out=t0[:, :, :], in0=px[0:C, :, :], scalar=0.0, in1=t2[:, :, :],
                                             op0=ALU.max, op1=ALU.add).then_inc(dve_sp, 1)
                    dve.wait_ge(dve_sp, count(dve_sp, G * 3 + 2))
                    dve.scalar_tensor_tensor(out=t1[:, :, :], in0=t0[:, :, :], scalar=0.5, in1=xcs[:, k % 4],
                                             op0=ALU.mult, op1=ALU.mult).then_inc(dve_sp, 1)

            def c_part(s, k, n):
                if n != AT["dve"]["y"]:
                    return
                G = s * NC8 + k
                dve.wait_ge(pe_red, count(pe_red, (G + 1) * NU))
                yy = xcs[:, k % 4]
                for t in range(2):
                    dve.scalar_tensor_tensor(out=yy[:, t, :], in0=xcs[:, k % 4, t, :], scalar=dhalf[:, t:t + 1],
                                             in1=py[0:C, t, :], op0=ALU.mult, op1=ALU.add).then_inc(dve_y, 1)
                dve.wait_ge(dve_zs, count(dve_zs, G + 1))
                dve.wait_ge(dve_y, count(dve_y, G * 3 + 2))
                dve.tensor_tensor(yy, yy, zs[:, :, :], ALU.mult).then_inc(dve_y, 1)

            run(nc.vector, MULT["dve"], LAG["dve"], unit, step, begin, a_part, c_part)

        @block.gpsimd
        def _(pool):
            pool.wait_ge(zset, count(zset, 3))

            def step(st, i):
                name = st.plan[i][1][0]
                if name in ("SG2", "DG2"):
                    v = int(name == "DG2")
                    x = stage_sample(st, name)
                    pool.wait_ge(cb_free[(i) % 2], st.freed(i))
                    if v:
                        pool.wait_ge(act_gn, count(act_gn, x))
                    gn = gn1 if v else gnx
                    pool.tensor_tensor(gn[:, 0:1], ve[:, v:v + 1], mhalf[:, :], ALU.pow)\
                        .then_inc(pool_d if v else pool_s, 1)

            def unit(s, k, n):
                G = s * NC8 + k
                q, j = n // NJ, n % NJ
                if j == 0:
                    pool.wait_ge(act_c, count(act_c, G * NQ + q + 1))
                pool.wait_ge(dve_h, count(dve_h, G * NU + n + 1))
                pool.wait_ge(pe_red, count(pe_red, G * NU + n + 1 - NHC))
                pool.tensor_tensor(hc[:, n % NHC, :], bu[:, n // 2 % 4, n % 2, :], cs[:, q % 2, :], ALU.mult)\
                    .then_inc(pool_hc, 1)
                if n % 2 == 1:
                    pool.tensor_copy(state[:, q, j - 1:j + 1], bu[:, n // 2 % 4, :, T - 1]).then_inc(pool_stt, 1)

            def a_part(s, k, n):
                G = s * NC8 + k
                if n == AT["pool"]["sp1"]:
                    pool.wait_ge(dve_sp, count(dve_sp, G * 3 + 1))
                    pool.tensor_tensor(t2[:, :, :], t2[:, :, :], t1[:, :, :], ALU.subtract).then_inc(pool_sp, 1)
                if n == AT["pool"]["sp2"]:
                    pool.wait_ge(pool_sp, count(pool_sp, G * 2 + 1))
                    pool.wait_ge(act_sp, count(act_sp, G * 3 + 3))
                    pool.tensor_tensor(t2[:, :, :], t0[:, :, :], t2[:, :, :], ALU.subtract).then_inc(pool_sp, 1)

            run(nc.gpsimd, MULT["pool"], LAG["pool"], unit, step, lambda st: None, a_part, lambda s, k, n: None)


def resampling():
    k = np.arange(-31, 32)

    def up(n):
        j, w = np.arange(n)[:, None], np.arange(64)[None, :]
        a = np.exp(2j * np.pi * k * (j / n - w / 64)[..., None]).sum(-1).real
        return (a + 2 * np.cos(2 * np.pi * 32 * j / n) * (-1.0) ** w) / 64

    def down(n):
        i, j = np.arange(64)[:, None], np.arange(n)[None, :]
        a = np.exp(2j * np.pi * k * (i / 64 - j / n)[..., None]).sum(-1).real
        return (a + np.cos(2 * np.pi * 32 * j / n) * (-1.0) ** i) / n

    up_w = np.zeros((128, 2, GW), np.float32)
    up_h = np.zeros((128, 2 * GH), np.float32)
    for r in range(2):
        up_w[64 * r:64 * r + 64, r] = up(GW).T
        up_h[64 * r:64 * r + 64, GH * r:GH * r + GH] = up(GH).T
    dn_w = np.zeros((GW, 96), np.float32)
    dn_w[:, 0:64] = down(GW).T
    return up_w, up_h, down(GH).T.astype(np.float32), dn_w


def selectors():
    sel = np.zeros((96, 2 * NQ, 128), np.float32)
    for q in range(2 * NQ):
        for m in range(128):
            for part in range(3):
                sel[32 * part + 4 * q + m // 32, q, m] = 1
    rsel = np.tile(np.eye(32, dtype=np.float32), (4, 1))
    return sel.reshape(96, -1), rsel


def kernel(**inputs):
    import concourse.bacc as bacc
    from concourse.bass_utils import run_bass_kernel_spmd

    g = {k: np.asarray(v) for k, v in inputs.items()}
    up_w, up_h, dn_h, dn_w = resampling()
    sel, rsel = selectors()
    wx = g["L1_conv_W_x"]
    arrays = {
        "x": g["x"],
        "W1": g["L0_conv_W1"], "W1T": g["L0_conv_W1"].T, "b1": g["L0_conv_b1"].reshape(NF, 128).T,
        "W2T": g["L0_conv_W2"].T, "b2": g["L0_conv_b2"], "coef": g["L0_conv_coef"],
        "WinT": g["L1_conv_W_in"].T, "conv_w": g["L1_conv_conv_w"].reshape(2, C, 3).transpose(1, 0, 2),
        "conv_b": g["L1_conv_conv_b"].reshape(2, C).T,
        "WxT": np.concatenate([wx[RANK:], wx[:RANK]], 0).T, "WdtT": g["L1_conv_W_dt"].T,
        "b_dt": g["L1_conv_b_dt"], "D": g["L1_conv_D"].reshape(2, C).T, "WoT": g["L1_conv_W_out"].T,
        "A_lay": g["L1_conv_A_log"].reshape(NJ, 32, NQ, 4).transpose(3, 1, 2, 0).reshape(128, NQ, NJ),
        "up_w": up_w, "up_h": up_h, "dn_h": dn_h, "dn_w": dn_w, "sel": sel, "rsel": rsel,
        "ident": np.eye(128, dtype=np.float32),
        "gavg": np.kron(np.eye(C // GROUP), np.full((GROUP, GROUP), 1.0 / GROUP)).astype(np.float32),
    }
    arrays = {f"in_{k}": np.ascontiguousarray(v) for k, v in arrays.items()}
    nc = bacc.Bacc("TRN2", target_bir_lowering=False, num_devices=1)
    aps = {k[3:]: nc.dram_tensor(k, a.shape, mybir.dt.from_np(a.dtype), kind="ExternalInput").ap()
           for k, a in arrays.items()}
    aps["out"] = nc.dram_tensor("out", (NS, HH, WW, C), F32, kind="ExternalOutput").ap()
    build(nc, aps)
    r = run_bass_kernel_spmd(nc, [arrays], core_ids=[0])
    return r.results[0]["out"]
```
